# Optimizing a Trainium2 kernel written in Bass

```python
import numpy as np
import jax
import jax.numpy as jnp

def _softmax(x, axis=-1):
    return jax.nn.softmax(x, axis=axis)

def _gelu(x):
    return jax.nn.gelu(x, approximate=True)

def _silu(x):
    return jax.nn.silu(x)

def _sigmoid(x):
    return jax.nn.sigmoid(x)

def _layernorm(x, axis=-1, eps=1e-05):
    m = jnp.mean(x, axis=axis, keepdims=True)
    v = jnp.var(x, axis=axis, keepdims=True)
    return (x - m) / jnp.sqrt(v + eps)

def _scatter_add(tgt, idx, src, axis=0):
    return tgt.at[idx].add(src)

def _segment_sum(src, seg, n):
    return jax.ops.segment_sum(src, seg, n)
kernel_name = 'mk_adj_resnorm_d1_adj_r2_1de125'

def setup_inputs(seed: int=0):
    np.random.seed(seed)
    _w = jnp.asarray

    def _rec_inputs():
        import jax
        import jax.numpy as jnp
        _gk = jax.random.key(seed)
        x = -0.0005207 + 1.001 * jax.random.normal(jax.random.fold_in(_gk, 1), (2048, 256), jnp.float32)
        _a = jax.random.bernoulli(jax.random.fold_in(_gk, 2), 0.0078125, (2048, 2048))
        adj = _a.astype(jnp.int32)
        return (x, adj)
    x, adj = _rec_inputs()

    def _L0_gnn_setup():
        import jax, jax.numpy as jnp
        import numpy as np
        N = 2048
        STATE_DIM = 256
        OUTPUT_DIM = 256
        N_STEPS = 5
        W_STD = 0.02

        def _lin_params(key, out_dim, in_dim):
            W = jax.random.normal(key, (out_dim, in_dim), dtype=jnp.float32) * W_STD
            b = jnp.zeros((out_dim,), dtype=jnp.float32)
            return (W, b)
        key = jax.random.key(seed)
        ks = jax.random.split(key, 10)
        prop_state = jax.random.normal(ks[0], (N, STATE_DIM), dtype=jnp.float32)
        A = jax.random.randint(ks[1], (N, N), 0, 2, dtype=jnp.int64)
        in_W, in_b = _lin_params(ks[2], STATE_DIM, STATE_DIM)
        out_W, out_b = _lin_params(ks[3], STATE_DIM, STATE_DIM)
        r_W, r_b = _lin_params(ks[4], STATE_DIM, 3 * STATE_DIM)
        z_W, z_b = _lin_params(ks[5], STATE_DIM, 3 * STATE_DIM)
        h_W, h_b = _lin_params(ks[6], STATE_DIM, 3 * STATE_DIM)
        o1_W, o1_b = _lin_params(ks[7], STATE_DIM, STATE_DIM)
        o2_W, o2_b = _lin_params(ks[8], OUTPUT_DIM, STATE_DIM)
        return {'prop_state': prop_state, 'A': A, 'in_W': in_W, 'in_b': in_b, 'out_W': out_W, 'out_b': out_b, 'r_W': r_W, 'r_b': r_b, 'z_W': z_W, 'z_b': z_b, 'h_W': h_W, 'h_b': h_b, 'o1_W': o1_W, 'o1_b': o1_b, 'o2_W': o2_W, 'o2_b': o2_b}
    _L0_gnn_all = _L0_gnn_setup()
    _L0_gnn_in = {k: v for k, v in _L0_gnn_all.items() if k in ('in_W', 'in_b', 'out_W', 'out_b', 'r_W', 'r_b', 'z_W', 'z_b', 'h_W', 'h_b', 'o1_W', 'o1_b', 'o2_W', 'o2_b')}
    del _L0_gnn_all
    return {'x': x, 'adj': adj, 'L0_gnn_in_W': _L0_gnn_in['in_W'], 'L0_gnn_in_b': _L0_gnn_in['in_b'], 'L0_gnn_out_W': _L0_gnn_in['out_W'], 'L0_gnn_out_b': _L0_gnn_in['out_b'], 'L0_gnn_r_W': _L0_gnn_in['r_W'], 'L0_gnn_r_b': _L0_gnn_in['r_b'], 'L0_gnn_z_W': _L0_gnn_in['z_W'], 'L0_gnn_z_b': _L0_gnn_in['z_b'], 'L0_gnn_h_W': _L0_gnn_in['h_W'], 'L0_gnn_h_b': _L0_gnn_in['h_b'], 'L0_gnn_o1_W': _L0_gnn_in['o1_W'], 'L0_gnn_o1_b': _L0_gnn_in['o1_b'], 'L0_gnn_o2_W': _L0_gnn_in['o2_W'], 'L0_gnn_o2_b': _L0_gnn_in['o2_b']}

def reference(x, adj, L0_gnn_in_W, L0_gnn_in_b, L0_gnn_out_W, L0_gnn_out_b, L0_gnn_r_W, L0_gnn_r_b, L0_gnn_z_W, L0_gnn_z_b, L0_gnn_h_W, L0_gnn_h_b, L0_gnn_o1_W, L0_gnn_o1_b, L0_gnn_o2_W, L0_gnn_o2_b):
    import jax
    import jax.numpy as jnp

    def _L0_gnn_ref(prop_state, A, in_W, in_b, out_W, out_b, r_W, r_b, z_W, z_b, h_W, h_b, o1_W, o1_b, o2_W, o2_b):
        import jax, jax.numpy as jnp
        import numpy as np
        N = 2048
        STATE_DIM = 256
        OUTPUT_DIM = 256
        N_STEPS = 5
        W_STD = 0.02

        def _lin_params(key, out_dim, in_dim):
            W = jax.random.normal(key, (out_dim, in_dim), dtype=jnp.float32) * W_STD
            b = jnp.zeros((out_dim,), dtype=jnp.float32)
            return (W, b)
        Af = A.astype(prop_state.dtype)
        AfT = Af.T
        state = prop_state
        for _ in range(N_STEPS):
            s_in = state @ in_W.T + in_b
            s_out = state @ out_W.T + out_b
            a_in = Af @ s_in
            a_out = AfT @ s_out
            a = jnp.concatenate([a_in, a_out, state], axis=-1)
            r = jax.nn.sigmoid(a @ r_W.T + r_b)
            z = jax.nn.sigmoid(a @ z_W.T + z_b)
            joined = jnp.concatenate([a_in, a_out, r * state], axis=-1)
            h_hat = jnp.tanh(joined @ h_W.T + h_b)
            state = (1.0 - z) * state + z * h_hat
        out = jnp.tanh(state @ o1_W.T + o1_b) @ o2_W.T + o2_b
        return out
    x = _layernorm(x + _L0_gnn_ref(x, adj, L0_gnn_in_W, L0_gnn_in_b, L0_gnn_out_W, L0_gnn_out_b, L0_gnn_r_W, L0_gnn_r_b, L0_gnn_z_W, L0_gnn_z_b, L0_gnn_h_W, L0_gnn_h_b, L0_gnn_o1_W, L0_gnn_o1_b, L0_gnn_o2_W, L0_gnn_o2_b), axis=-1)
    return x

_drawn_inputs = setup_inputs


def setup_inputs(seed=0):
    import zlib

    import numpy as np

    out = dict(_drawn_inputs(seed))
    spreads = {'L0_gnn_in_b': (0.0, 0.1),
     'L0_gnn_out_b': (0.0, 0.1),
     'L0_gnn_r_b': (0.0, 0.8),
     'L0_gnn_z_b': (0.0, 0.8),
     'L0_gnn_h_b': (0.0, 0.797),
     'L0_gnn_o1_b': (0.0, 0.1),
     'L0_gnn_o2_b': (0.0, 0.1)}
    factors = {'L0_gnn_r_W': 8.0}
    for name, (base, spread) in spreads.items():
        noise = np.random.default_rng([zlib.crc32(name.encode()), seed]).standard_normal(out[name].shape)
        drawn = base * np.exp(spread * noise) if base else spread * noise
        out[name] = jnp.asarray(drawn.astype(out[name].dtype))
    for name, factor in factors.items():
        out[name] = (out[name] * factor).astype(out[name].dtype)
    return out
```

```python
import concourse.bass as bass
from concourse import mybir
from contextlib import ExitStack

F32 = mybir.dt.float32
F16 = mybir.dt.float16
F8 = mybir.dt.float8e4
I32 = mybir.dt.int32
U32 = mybir.dt.uint32
ACT = mybir.ActivationFunctionType
ALU = mybir.AluOpType
AX = mybir.AxisListType.X
RMAX = bass.bass_isa.ReduceOp.max

P = 128
N = 2048
D = 256
STEPS = 5
FT = D // P
JT = N // P
CW = 512
CH = N // CW
JC = CW // P
KT = 3 * FT
GD = 3 * D
GT = GD // P
STG = 3
JH = JT - JC

TOP = 2.0 ** 14
SIG_READY = 5
PSC = 1.0 / N
EXP_BITS = 0x7F800000
LN_EPS = 1e-5
PASSES = ((0, 0), (0, 1), (1, 0))


def gnn_program(nc, x, x_t, adj, adj_t, io_w, gate_w, o_w, bias, o2_b, out):
    ctx = ExitStack()
    with ctx:
        def sb(name, shape, dt):
            return ctx.enter_context(nc.sbuf_tensor(name, shape, dt))

        def sem(name):
            return ctx.enter_context(nc.semaphore(name))

        a8 = sb("a8", [P, JT, N], F8)
        at_words = sb("at_words", [P, JT * N // 4], F32)
        at8 = at_words[:, :].bitcast(F8).rearrange("p (j n) -> p j n", j=JT)
        x_nat = at_words[:, JT * N // 8:].rearrange("p (j f) -> p j f", f=D)
        state_n = sb("state_n", [P, JT, 2, D], F16)
        state_t = sb("state_t", [P, FT, N], F32)
        split_t = sb("split_t", [P, 2, FT, N], F16)
        w16 = sb("w16", [P, KT, 2, GD], F16)
        o16 = sb("o16", [P, FT, 2, 2 * D], F16)

        pq_words = sb("pq_words", [P, CH * 2 * FT * CW], F32)
        pq = pq_words[:, :].bitcast(F16).rearrange("p (c q s n) -> p c q s n", c=CH, q=2 * FT, s=2)
        slot_words = 2 * FT * CW
        gw = pq_words[:, 0:KT * GD].rearrange("p (k m) -> p k m", k=KT)
        fold = pq_words[:, KT * GD:KT * GD + 2 * FT * GD].rearrange("p (k m) -> p k m", k=2 * FT)
        next_n = pq_words[:, slot_words:slot_words + JH * D].bitcast(F16) \
            .rearrange("p (j s f) -> p j s f", j=JH, s=2)
        y = pq_words[:, 3 * slot_words:4 * slot_words].rearrange("p (b j f) -> p b j f", b=2, j=JC)
        hid = pq_words[:, slot_words:slot_words + FT * CW].rearrange("p (k n) -> p k n", k=FT)
        hid16 = pq_words[:, slot_words + FT * CW:slot_words + 2 * FT * CW].bitcast(F16) \
            .rearrange("p (k s n) -> p k s n", k=FT, s=2)

        deg_words = sb("deg_words", [P, 2 * N // 2], F32)
        deg = deg_words[:, :].bitcast(F16).rearrange("p (d n) -> p d n", d=2)
        iow = deg_words[:, 0:2 * FT * D].rearrange("p (k m) -> p k m", k=2 * FT)
        ow = deg_words[:, 2 * FT * D:].rearrange("p (k m) -> p k m", k=FT)
        diag_words = sb("diag_words", [P, 2 * JT * P // 2], F32)
        diag = diag_words[:, :].bitcast(F16).rearrange("p (d j m) -> p d j m", d=2, j=JT)
        b2_all = diag_words[:, 0:D]

        tmp = sb("tmp", [P, STG * N], F32)
        stage = tmp[:, :].bitcast(I32).rearrange("p (s n) -> p s n", s=STG)
        pre = tmp[:, 0:3 * CW].rearrange("p (b n) -> p b n", b=3)
        r_buf = tmp[:, 3 * CW:5 * CW].rearrange("p (f n) -> p f n", f=FT)
        z_buf = tmp[:, 5 * CW:7 * CW].rearrange("p (f n) -> p f n", f=FT)
        h_buf = tmp[:, 7 * CW:9 * CW].rearrange("p (f n) -> p f n", f=FT)
        rs16 = tmp[:, 9 * CW:11 * CW].bitcast(F16).rearrange("p (s f n) -> p s f n", s=2, f=FT)

        ident = sb("ident", [P, P], F16)
        ones = sb("ones", [P, P], F16)
        bias_sb = sb("bias_sb", [P, 12], F32)
        degc = sb("degc", [P, 2, JT], F32)
        vdeg = sb("vdeg", [P, 2, GT], F32)
        mx = sb("mx", [P, 12], F32)
        mall = sb("mall", [P, 6], F32)
        scal = sb("scal", [P, 12], F32)
        ln_st = sb("ln_st", [P, JC, 6], F32)
        ln_mv = sb("ln_mv", [P, JC, 2], F32)
        ln_t = sb("ln_t", [P, 4, JC], F32)

        PX, SIG, PW, OMG, OMGP, UG, UO1, UO2, OM1, OM2, T0, T1 = [scal[:, i:i + 1] for i in range(12)]

        bank = [ctx.enter_context(nc.psum_tensor(f"bank{i}", [P, CW], F32)) for i in range(8)]
        gate_bank = bank[4:7]
        tr_bank = bank[7]
        tr16 = tr_bank[:, :].bitcast(F16).rearrange("p (j s f) -> p j s f", j=JC, s=2)

        s_iow, s_gwp, s_gws, s_xt, s_ow, s_bias, s_b2 = [
            sem(n) for n in ("s_iow", "s_gwp", "s_gws", "s_xt", "s_ow", "s_bias", "s_b2")]
        s_x = [sem(f"s_x{c}") for c in range(CH)]
        s_adj = [sem(f"s_adj{i}") for i in range(STG)]
        s_cast = sem("s_cast")
        s_const0, s_const = sem("s_const0"), sem("s_const")
        s_mx, s_mall = sem("s_mx"), sem("s_mall")
        s_sc = sem("s_sc")
        s_snh, s_snl = sem("s_snh"), sem("s_snl")
        s_fold, s_fev = sem("s_fold"), sem("s_fev")
        s_wh, s_wl = sem("s_wh"), sem("s_wl")
        s_q0, s_q0h, s_q0l = sem("s_q0"), sem("s_q0h"), sem("s_q0l")
        s_p0, s_p0h, s_p0l = sem("s_p0"), sem("s_p0h"), sem("s_p0l")
        s_diag, s_dg, s_deg = sem("s_diag"), sem("s_dg"), sem("s_deg")
        s_pq, s_pqh, s_pql = sem("s_pq"), sem("s_pqh"), sem("s_pql")
        s_gate = sem("s_gate")
        s_gfree = sem("s_gfree")
        s_pre = sem("s_pre")
        s_act = sem("s_act")
        s_rs, s_rsh, s_rsl = sem("s_rs"), sem("s_rsh"), sem("s_rsl")
        s_d, s_zd, s_new = sem("s_d"), sem("s_zd"), sem("s_new")
        s_sh, s_sl = sem("s_sh"), sem("s_sl")
        s_tr, s_nat = sem("s_tr"), sem("s_nat")
        s_cur = sem("s_cur")
        s_o1, s_hid, s_hh, s_hl = sem("s_o1"), sem("s_hid"), sem("s_hh"), sem("s_hl")
        s_o2, s_y, s_ln, s_norm = sem("s_o2"), sem("s_y"), sem("s_ln"), sem("s_norm")
        s_xr = [sem("s_xr0"), sem("s_xr1")]
        s_xb = sem("s_xb")
        s_out = [sem("s_out0"), sem("s_out1")]

        def cols(c):
            return slice(c * CW, (c + 1) * CW)

        def feat(f):
            return slice(f * P, (f + 1) * P)

        def p0_bank(c, f):
            return (2 * FT + 2 * c + f) % 8

        def store_rows(sp, c):
            sp.wait_ge(s_norm, JC * (c + 1))
            sp.dma_start(out.rearrange("(j p) f -> p j f", p=P)[:, c * JC:(c + 1) * JC, :], y[:, c % 2, :, :]) \
                .then_inc(s_out[c % 2], 16)

        block = ctx.enter_context(nc.Block())

        @block.sync
        def _(sp):
            io_v = io_w.rearrange("(k p) m -> p k m", p=P)
            gw_v = gate_w.rearrange("(k p) m -> p k m", p=P)
            x_v = x.rearrange("(j p) f -> p j f", p=P)
            sp.dma_start(bias_sb[:, :], bias).then_inc(s_bias, 16)
            sp.dma_start(iow, io_v).then_inc(s_iow, 16)
            sp.dma_start(gw[:, 0:2 * FT, :], gw_v[:, 0:2 * FT, :]).then_inc(s_gwp, 16)
            for c in range(CH):
                sp.dma_start(x_nat[:, c * JC:(c + 1) * JC, :], x_v[:, c * JC:(c + 1) * JC, :]) \
                    .then_inc(s_x[c], 16)

            def load_rows(k):
                src = adj if k < JT else adj_t
                if k >= STG:
                    sp.wait_ge(s_cast, k - STG + 1)
                sp.dma_start(stage[:, k % STG, :], src[(k % JT) * P:(k % JT + 1) * P, :]) \
                    .then_inc(s_adj[k % STG], 16)

            for k in range(STG):
                load_rows(k)
            sp.dma_start(gw[:, 2 * FT:, :], gw_v[:, 2 * FT:, :]).then_inc(s_gws, 16)
            sp.dma_start(ow, o_w.rearrange("(k p) m -> p k m", p=P)).then_inc(s_ow, 16)
            sp.dma_start(state_t[:, :, :], x_t.rearrange("(f p) n -> p f n", p=P)).then_inc(s_xt, 16)
            for k in range(STG, 2 * JT):
                load_rows(k)

            sp.wait_ge(s_dg, 8)
            sp.dma_start(b2_all, o2_b.partition_broadcast(P)).then_inc(s_b2, 16)
            sp.wait_ge(s_gate, GT * CH)
            for c in range(CH):
                if c >= 2:
                    sp.wait_ge(s_out[c % 2], 16)
                sp.dma_start(y[:, c % 2, :, :], x_v[:, c * JC:(c + 1) * JC, :]).then_inc(s_xr[c % 2], 16)
                if c >= 1:
                    store_rows(sp, c - 1)
            store_rows(sp, CH - 1)
            sp.wait_ge(s_out[0], 16 * CH // 2)
            sp.wait_ge(s_out[1], 16 * CH // 2)

        @block.gpsimd
        def _(pool):
            nc.gpsimd.memset(ident[:, :], 0.0).then_inc(s_const0, 1)
            nc.gpsimd.memset(ones[:, :], 1.0).then_inc(s_const, 1)
            pool.wait_ge(s_const0, 1)
            nc.gpsimd.affine_select(out=ident[:, :], in_=ident[:, :], compare_op=ALU.not_equal, fill=1.0, base=0,
                                    pattern=[[-1, P]], channel_multiplier=1).then_inc(s_const, 1)
            pool.wait_ge(s_mx, 1)
            nc.gpsimd.partition_all_reduce(mall[:, 0:1], mx[:, 0:1], P, RMAX).then_inc(s_mall, 1)
            pool.wait_ge(s_mx, 2)
            nc.gpsimd.partition_all_reduce(mall[:, 1:5], mx[:, 1:5], P, RMAX).then_inc(s_mall, 1)
            pool.wait_ge(s_b2, 16)
            for c in range(CH):
                pool.wait_ge(s_xr[c % 2], 16 * (c // 2 + 1))
                for j in range(JC):
                    last = nc.gpsimd.tensor_tensor(y[:, c % 2, j, :], y[:, c % 2, j, :], b2_all, ALU.add)
                last.then_inc(s_xb, 1)

        @block.scalar
        def _(act):
            for o in range(2 * FT):
                act.wait_ge(s_fold, 2 * (o // 2) + 2)
                nc.scalar.copy(fold[:, o, 0:CW], bank[o][:, :])
                nc.scalar.copy(fold[:, o, CW:GD], bank[4 + o // 2][:, (o % 2) * D:(o % 2 + 1) * D]) \
                    .then_inc(s_fev, 1)
            act.wait_ge(s_fold, 2 * FT + 1)
            nc.scalar.copy(vdeg[:, :, :], bank[6][:, 0:2 * GT].rearrange("p (d m) -> p d m", d=2)).then_inc(s_fev, 1)
            act.wait_ge(s_sc, SIG_READY)
            for c in range(CH):
                nc.scalar.activation(state_n[:, c * JC:(c + 1) * JC, 0, :], x_nat[:, c * JC:(c + 1) * JC, :],
                                     ACT.Copy, scale=SIG).then_inc(s_snh, 1)

            def cast_rows(k):
                act.wait_ge(s_adj[k % STG], 16 * (k // STG + 1))
                if k == JT + JT // 2:
                    act.wait_ge(s_snl, CH)
                dst = a8 if k < JT else at8
                nc.scalar.activation(dst[:, k % JT, :], stage[:, k % STG, :], ACT.Copy,
                                     accum_out=degc[:, k // JT, k % JT:k % JT + 1], saturate=False) \
                    .then_inc(s_cast, 1)

            for k in range(JT):
                cast_rows(k)
            act.wait_ge(s_wl, 2)
            for c in range(CH):
                for f in range(FT):
                    act.wait_ge(s_q0, 2 * c + f + 1)
                    nc.scalar.activation(pq[:, c, FT + f, 0, :], bank[2 * c + f][:, :], ACT.Copy, scale=PSC) \
                        .then_inc(s_q0h, 1)
                cast_rows(JT + c)
            for k in range(JT + CH, 2 * JT):
                cast_rows(k)
            for c in range(CH):
                for f in range(FT):
                    act.wait_ge(s_p0, 2 * c + f + 1)
                    nc.scalar.activation(pq[:, c, f, 0, :], bank[p0_bank(c, f)][:, :], ACT.Copy, scale=PSC) \
                        .then_inc(s_p0h, 1)

            def pq_hi(n, q):
                act.wait_ge(s_pq, 4 * (n - CH) + q + 1)
                nc.scalar.activation(pq[:, 0, q, 0, :], bank[q][:, :], ACT.Copy, scale=PSC).then_inc(s_pqh, 1)

            def nat_out(n, c, f, direct):
                dst = state_n if direct or c == CH - 1 else next_n
                act.wait_ge(s_tr, 2 * n + f + 1)
                nc.scalar.copy(dst[:, c * JC:(c + 1) * JC, :, feat(f)], tr16).then_inc(s_nat, 1)

            def gate_act(n, gi):
                dst = (r_buf, z_buf, h_buf)[gi // FT]
                act.wait_ge(s_pre, GT * n + gi + 1)
                nc.scalar.activation(dst[:, gi % FT, :], pre[:, gi % 3, :], ACT.Tanh if gi >= 2 * FT else ACT.Sigmoid,
                                     bias=bias_sb[:, 4 + gi:5 + gi], scale=UG).then_inc(s_act, 1)

            def gates(n, c, between=()):
                gate_act(n, 0)
                gate_act(n, 1)
                for f in range(FT):
                    act.wait_ge(s_rs, FT * n + f + 1)
                    nc.scalar.activation(rs16[:, 0, f, :], r_buf[:, f, :], ACT.Copy, scale=SIG).then_inc(s_rsh, 1)
                gate_act(n, 2)
                gate_act(n, 3)
                for f in between:
                    nat_out(n - 1, c - 1, f, True)
                gate_act(n, 4)
                gate_act(n, 5)
                for f in range(FT):
                    act.wait_ge(s_new, FT * n + f + 1)
                    nc.scalar.activation(split_t[:, 0, f, cols(c)], state_t[:, f, cols(c)], ACT.Copy, scale=SIG) \
                        .then_inc(s_sh, 1)

            def head_act(c):
                for m in range(FT):
                    act.wait_ge(s_o1, FT * c + m + 1)
                    nc.scalar.activation(hid[:, m, :], bank[4 + m][:, :], ACT.Tanh,
                                         bias=bias_sb[:, 10 + m:11 + m], scale=UO1).then_inc(s_hid, 1)
                for m in range(FT):
                    act.wait_ge(s_hid, FT * c + m + 1)
                    nc.scalar.activation(hid16[:, m, 0, :], hid[:, m, :], ACT.Copy, scale=TOP).then_inc(s_hh, 1)

            def step(t, last, first_direct):
                for c in range(CH):
                    n = CH * t + c
                    if c == 0:
                        nat_out(n - 1, CH - 1, 0, first_direct)
                        nat_out(n - 1, CH - 1, 1, first_direct)
                    pq_hi(n, 0)
                    if c > 0 and not last:
                        nat_out(n - 1, c - 1, 0, False)
                    if c > 0 and last:
                        head_act(c - 1)
                    pq_hi(n, 1)
                    if c > 0 and not last:
                        nat_out(n - 1, c - 1, 1, False)
                    pq_hi(n, 2)
                    pq_hi(n, 3)
                    gates(n, c)
                if last:
                    head_act(CH - 1)

            for c in range(CH):
                gates(c, c, between=range(FT) if c else ())
            with act.Fori(1, STEPS - 1) as t:
                step(t, False, True)
            step(STEPS - 1, True, True)

        @block.vector
        def _(dve):
            chain = [0]

            def link(ins):
                chain[0] += 1
                ins.then_inc(s_sc, 1)
                dve.wait_ge(s_sc, chain[0])

            for c in range(CH):
                dve.wait_ge(s_x[c], 16)
                last = nc.vector.tensor_reduce(mx[:, 8 + c:9 + c], x_nat[:, c * JC:(c + 1) * JC, :],
                                               mybir.AxisListType.XY, ALU.max, apply_absolute_value=True)
            link(last)
            nc.vector.tensor_reduce(mx[:, 0:1], mx[:, 8:12], AX, ALU.max).then_inc(s_mx, 1)
            dve.wait_ge(s_mall, 1)
            link(nc.vector.tensor_scalar(T0, mall[:, 0:1], 1.0, None, ALU.max))
            link(nc.vector.tensor_scalar(PX.bitcast(U32), T0.bitcast(U32), EXP_BITS, None, ALU.bitwise_and))
            link(nc.vector.reciprocal(T1, PX))
            link(nc.vector.tensor_scalar(SIG, T1, TOP, None, ALU.mult))
            assert chain[0] == SIG_READY
            for c in range(CH):
                dve.wait_ge(s_snh, c + 1)
                nc.vector.scalar_tensor_tensor(state_n[:, c * JC:(c + 1) * JC, 1, :], x_nat[:, c * JC:(c + 1) * JC, :],
                                               SIG, state_n[:, c * JC:(c + 1) * JC, 0, :], ALU.mult, ALU.subtract) \
                    .then_inc(s_snl, 1)
            dve.wait_ge(s_fev, 2 * FT)
            nc.vector.tensor_reduce(mx[:, 1:2], fold, mybir.AxisListType.XY, ALU.max, apply_absolute_value=True)
            dve.wait_ge(s_gws, 16)
            nc.vector.tensor_reduce(mx[:, 2:3], gw[:, 2 * FT:, :], mybir.AxisListType.XY, ALU.max,
                                    apply_absolute_value=True)
            dve.wait_ge(s_ow, 16)
            nc.vector.tensor_reduce(mx[:, 3:4], ow[:, :, 0:D], mybir.AxisListType.XY, ALU.max,
                                    apply_absolute_value=True)
            nc.vector.tensor_reduce(mx[:, 4:5], ow[:, :, D:2 * D], mybir.AxisListType.XY, ALU.max,
                                    apply_absolute_value=True).then_inc(s_mx, 1)
            dve.wait_ge(s_mall, 2)
            link(nc.vector.tensor_scalar(T0, mall[:, 1:2], 1.0 / PSC, 1e-30, ALU.mult, ALU.max))
            link(nc.vector.tensor_tensor(T1, T0, mall[:, 2:3], ALU.max))
            link(nc.vector.tensor_scalar(PW.bitcast(U32), T1.bitcast(U32), EXP_BITS, None, ALU.bitwise_and))
            link(nc.vector.reciprocal(T0, PW))
            link(nc.vector.tensor_scalar(OMG, T0, TOP, None, ALU.mult))
            link(nc.vector.tensor_scalar(OMGP, T0, TOP / PSC, None, ALU.mult))
            link(nc.vector.tensor_scalar(UG, PW, PX, 1.0 / (TOP * TOP), ALU.mult, ALU.mult))
            for src, om, un in ((mall[:, 3:4], OM1, UO1), (mall[:, 4:5], OM2, UO2)):
                link(nc.vector.tensor_scalar(T0, src, 1e-30, None, ALU.max))
                link(nc.vector.tensor_scalar(un.bitcast(U32), T0.bitcast(U32), EXP_BITS, None, ALU.bitwise_and))
                link(nc.vector.reciprocal(T1, un))
                link(nc.vector.tensor_scalar(om, T1, TOP, None, ALU.mult))
            link(nc.vector.tensor_scalar(T0, UO1, PX, 1.0 / (TOP * TOP), ALU.mult, ALU.mult))
            link(nc.vector.tensor_copy(UO1, T0))
            link(nc.vector.tensor_scalar(T1, UO2, 1.0 / (TOP * TOP), None, ALU.mult))
            link(nc.vector.tensor_copy(UO2, T1))
            dve.wait_ge(s_fev, 2 * FT + 1)
            link(nc.vector.tensor_scalar(vdeg[:, :, :], vdeg[:, :, :], SIG, OMG, ALU.mult, ALU.mult))
            parts = ((w16[:, 0:2 * FT, :, :], fold, OMGP), (w16[:, 2 * FT:, :, :], gw[:, 2 * FT:, :], OMG),
                     (o16[:, :, :, 0:D], ow[:, :, 0:D], OM1), (o16[:, :, :, D:2 * D], ow[:, :, D:2 * D], OM2))
            for i, (dst, src, om) in enumerate(parts):
                nc.vector.tensor_scalar(dst[:, :, 0, :], src, om, None, ALU.mult).then_inc(s_wh, 1)
                dve.wait_ge(s_wh, i + 1)
                nc.vector.scalar_tensor_tensor(dst[:, :, 1, :], src, om, dst[:, :, 0, :], ALU.mult, ALU.subtract) \
                    .then_inc(s_wl, 1)
            dve.wait_ge(s_xt, 16)
            nc.vector.tensor_scalar(split_t[:, 0, :, :], state_t[:, :, :], SIG, None, ALU.mult).then_inc(s_wh, 1)
            dve.wait_ge(s_wh, 5)
            nc.vector.scalar_tensor_tensor(split_t[:, 1, :, :], state_t[:, :, :], SIG, split_t[:, 0, :, :],
                                           ALU.mult, ALU.subtract).then_inc(s_wl, 1)

            def lo_of_psum(c, q, src, done):
                return nc.vector.scalar_tensor_tensor(pq[:, c, q, 1, :], src[:, :], PSC, pq[:, c, q, 0, :],
                                                      ALU.mult, ALU.subtract).then_inc(done, 1)

            dve.wait_ge(s_const, 2)

            def make_diag(d):
                dve.wait_ge(s_cast, JT * (d + 1))
                for j in range(JT):
                    last = nc.vector.tensor_scalar(diag[:, d, j, :], ident[:, :], degc[:, d, j:j + 1], None, ALU.mult)
                last.then_inc(s_diag, 1)

            make_diag(0)
            for c in range(CH):
                for f in range(FT):
                    dve.wait_ge(s_q0h, 2 * c + f + 1)
                    lo_of_psum(c, FT + f, bank[2 * c + f], s_q0l)
            make_diag(1)

            def p0_lo(c):
                for f in range(FT):
                    dve.wait_ge(s_p0h, 2 * c + f + 1)
                    lo_of_psum(c, f, bank[p0_bank(c, f)], s_p0l)

            def deg_out(d):
                for c in range(CH):
                    dve.wait_ge(s_dg, CH * d + c + 1)
                    nc.vector.tensor_copy(deg[:, d, cols(c)], bank[4 + c][:, :]).then_inc(s_deg, 1)

            p0_lo(0)
            p0_lo(1)
            p0_lo(2)
            deg_out(0)
            p0_lo(3)
            deg_out(1)
            dve.wait_ge(s_deg, 2 * CH)

            def gate_pre(n, c, gi):
                g = GT * n + gi
                dve.wait_ge(s_gate, g + 1)
                if not (isinstance(n, int) and n == 0 and gi < 3):
                    dve.wait_ge(s_act, g - 2)
                nc.vector.scalar_tensor_tensor(pre[:, gi % 3, :], deg[:, 0, cols(c)], vdeg[:, 0, gi:gi + 1],
                                               gate_bank[gi % 3][:, :], ALU.mult, ALU.add).then_inc(s_gfree, 1)
                dve.wait_ge(s_gfree, g + 1)
                nc.vector.scalar_tensor_tensor(pre[:, gi % 3, :], deg[:, 1, cols(c)], vdeg[:, 1, gi:gi + 1],
                                               pre[:, gi % 3, :], ALU.mult, ALU.add).then_inc(s_pre, 1)

            def reset_part(n, c):
                for f in range(FT):
                    dve.wait_ge(s_act, GT * n + f + 1)
                    nc.vector.tensor_tensor(r_buf[:, f, :], r_buf[:, f, :], state_t[:, f, cols(c)], ALU.mult) \
                        .then_inc(s_rs, 1)
                for f in range(FT):
                    dve.wait_ge(s_rsh, FT * n + f + 1)
                    nc.vector.scalar_tensor_tensor(rs16[:, 1, f, :], r_buf[:, f, :], SIG, rs16[:, 0, f, :],
                                                   ALU.mult, ALU.subtract).then_inc(s_rsl, 1)

            def update(n, c):
                for f in range(FT):
                    k = FT * n + f + 1
                    dve.wait_ge(s_act, GT * n + 4 + f + 1)
                    nc.vector.tensor_tensor(h_buf[:, f, :], h_buf[:, f, :], state_t[:, f, cols(c)], ALU.subtract) \
                        .then_inc(s_d, 1)
                    dve.wait_ge(s_d, k)
                    nc.vector.tensor_tensor(z_buf[:, f, :], z_buf[:, f, :], h_buf[:, f, :], ALU.mult).then_inc(s_zd, 1)
                    dve.wait_ge(s_zd, k)
                    nc.vector.tensor_tensor(state_t[:, f, cols(c)], state_t[:, f, cols(c)], z_buf[:, f, :], ALU.add) \
                        .then_inc(s_new, 1)
                for f in range(FT):
                    k = FT * n + f + 1
                    dve.wait_ge(s_sh, k)
                    nc.vector.scalar_tensor_tensor(split_t[:, 1, f, cols(c)], state_t[:, f, cols(c)], SIG,
                                                   split_t[:, 0, f, cols(c)], ALU.mult, ALU.subtract) \
                        .then_inc(s_sl, 1)

            def gates(n, c, between=None):
                gate_pre(n, c, 0)
                gate_pre(n, c, 1)
                reset_part(n, c)
                gate_pre(n, c, 2)
                if between:
                    between()
                for gi in range(3, GT):
                    gate_pre(n, c, gi)
                update(n, c)

            def head_lo(c):
                for m in range(FT):
                    dve.wait_ge(s_hh, FT * c + m + 1)
                    nc.vector.scalar_tensor_tensor(hid16[:, m, 1, :], hid[:, m, :], TOP, hid16[:, m, 0, :],
                                                   ALU.mult, ALU.subtract).then_inc(s_hl, 1)

            def residual(c):
                dve.wait_ge(s_xb, c + 1)
                for h in range(2):
                    dve.wait_ge(s_o2, 2 * c + h + 1)
                    rows = y[:, c % 2, 2 * h:2 * h + 2, :]
                    nc.vector.scalar_tensor_tensor(rows, bank[6 + h][:, :].rearrange("p (j f) -> p j f", j=2), UO2,
                                                   rows, ALU.mult, ALU.add).then_inc(s_y, 1)

            ln_chain = [0]

            def ln_link(ins):
                ln_chain[0] += 1
                ins.then_inc(s_ln, 1)
                dve.wait_ge(s_ln, ln_chain[0])

            def layer_norm(c):
                dve.wait_ge(s_y, 2 * c + 2)
                for j in range(JC):
                    last = nc.vector.bn_stats(ln_st[:, j, :], y[:, c % 2, j, :])
                ln_link(last)
                for j in range(JC):
                    last = nc.vector.bn_aggr(ln_mv[:, j, :], ln_st[:, j, :])
                ln_link(last)
                var, a, b, r = [ln_t[:, i, :] for i in range(4)]
                ln_link(nc.vector.tensor_scalar(var, ln_mv[:, :, 1], LN_EPS, None, ALU.add))
                ln_link(nc.vector.tensor_scalar(a.bitcast(U32), var.bitcast(U32), 1, None, ALU.logical_shift_right))
                ln_link(nc.vector.tensor_scalar(r.bitcast(I32), a.bitcast(I32), -1.0, float(0x5F3759DF),
                                                ALU.mult, ALU.add))
                for _ in range(4):
                    ln_link(nc.vector.tensor_tensor(a, r, r, ALU.mult))
                    ln_link(nc.vector.scalar_tensor_tensor(b, a, -0.5, var, ALU.mult, ALU.mult))
                    ln_link(nc.vector.scalar_tensor_tensor(r, b, 1.5, r, ALU.add, ALU.mult))
                for j in range(JC):
                    nc.vector.tensor_scalar(y[:, c % 2, j, :], y[:, c % 2, j, :], ln_mv[:, j, 0:1], r[:, j:j + 1],
                                            ALU.subtract, ALU.mult).then_inc(s_norm, 1)

            def pq_lo(n, q):
                dve.wait_ge(s_pqh, 4 * (n - CH) + q + 1)
                lo_of_psum(0, q, bank[q], s_pql)

            def step(t, last):
                for c in range(CH):
                    n = CH * t + c
                    pq_lo(n, 0)
                    if last and c > 0:
                        head_lo(c - 1)
                    pq_lo(n, 1)
                    pq_lo(n, 2)
                    if last and c > 0:
                        residual(c - 1)
                    pq_lo(n, 3)
                    if c == CH - 1 and not last:
                        dve.wait_ge(s_nat, 2 * n)
                        nc.vector.tensor_copy(state_n[:, 0:JH, :, :], next_n).then_inc(s_cur, 1)
                    gates(n, c, (lambda: layer_norm(c - 1)) if last and c > 0 else None)
                if last:
                    head_lo(CH - 1)
                    residual(CH - 1)
                    layer_norm(CH - 1)

            for c in range(CH):
                gates(c, c)
            with dve.Fori(1, STEPS - 1) as t:
                step(t, False)
            step(STEPS - 1, True)

        @block.tensor
        def _(pe):
            pe.wait_ge(s_iow, 16)
            pe.wait_ge(s_gwp, 16)
            for o in range(2 * FT):
                d, k = o // FT, o % FT
                for dst, lo, hi in ((bank[o][:, :], 0, CW), (bank[4 + o // 2][:, (o % 2) * D:(o % 2 + 1) * D], CW, GD)):
                    for ct in range(FT):
                        last = nc.tensor.matmul(dst, iow[:, FT * d + ct, feat(k)], gw[:, FT * d + ct, lo:hi],
                                                start=ct == 0, stop=ct == FT - 1)
                last.then_inc(s_fold, 1)
            pe.wait_ge(s_bias, 16)
            for d in range(2):
                for m in range(GT):
                    for ct in range(FT):
                        last = nc.tensor.matmul(bank[6][:, d * GT + m:d * GT + m + 1], gw[:, FT * d + ct, feat(m)],
                                                bias_sb[:, FT * d + ct:FT * d + ct + 1],
                                                start=ct == 0, stop=ct == FT - 1)
            last.then_inc(s_fold, 1)

            def adj_mm(dst, adj8, j, part, f, c):
                return nc.tensor.matmul(dst[:, :], state_n[:, j, part, feat(f)], adj8[:, j, cols(c)],
                                        start=j == 0 and part == 0, stop=j == JT - 1 and part == 1)

            pe.wait_ge(s_fev, 2 * FT + 1)
            for j in range(JH):
                if j % JC == 0:
                    pe.wait_ge(s_snh, j // JC + 1)
                    pe.wait_ge(s_snl, j // JC + 1)
                pe.wait_ge(s_cast, j + 1)
                for f in range(FT):
                    for part in range(2):
                        for c in range(CH):
                            adj_mm(bank[2 * c + f], a8, j, part, f, c)
            pe.wait_ge(s_snh, CH)
            pe.wait_ge(s_snl, CH)
            pe.wait_ge(s_cast, JT)
            for c in range(CH):
                for f in range(FT):
                    for j in range(JH, JT):
                        for part in range(2):
                            last = adj_mm(bank[2 * c + f], a8, j, part, f, c)
                    last.then_inc(s_q0, 1)
            for j in range(JH):
                pe.wait_ge(s_cast, JT + j + 1)
                for c in (2, 3, 0, 1):
                    for f in range(FT):
                        if j == 0:
                            pe.wait_ge(s_q0h, p0_bank(c, f) + 1)
                            pe.wait_ge(s_q0l, p0_bank(c, f) + 1)
                        for part in range(2):
                            adj_mm(bank[p0_bank(c, f)], at8, j, part, f, c)
            pe.wait_ge(s_cast, 2 * JT)

            def spread_degrees(d):
                pe.wait_ge(s_diag, d + 1)
                for c in range(CH):
                    if d == 0:
                        pe.wait_ge(s_p0h, c + 1)
                        pe.wait_ge(s_p0l, c + 1)
                    else:
                        pe.wait_ge(s_deg, c + 1)
                    nc.tensor.matmul(bank[4 + c][:, :], ones[:, :], diag[:, d, c * JC:(c + 1) * JC, :],
                                     start=True, stop=True).then_inc(s_dg, 1)

            pe.wait_ge(s_const, 2)
            for c in range(CH):
                for f in range(FT):
                    for j in range(JH, JT):
                        for part in range(2):
                            last = adj_mm(bank[p0_bank(c, f)], at8, j, part, f, c)
                    last.then_inc(s_p0, 1)
                if c == CH - 2:
                    spread_degrees(0)
            spread_degrees(1)

            def products(n, c, q, tiles):
                for j in tiles:
                    for part in range(2):
                        last = adj_mm(bank[q], (at8, a8)[q // FT], j, part, q % FT, c)
                if tiles[-1] == JT - 1:
                    last.then_inc(s_pq, 1)

            def gate_tile(n, c, gi, slot, ready):
                dst = gate_bank[gi % 3]
                adj_k = [0, 1, 2, 3]
                state_k = [4, 5]
                order = state_k + adj_k if gi < 2 * FT else adj_k + state_k
                for i, k in enumerate(order):
                    if k < 2 * FT and gi == 0:
                        ready(k)
                    if k >= 2 * FT and gi == 2 * FT:
                        pe.wait_ge(s_rsh, FT * n + k - 2 * FT + 1)
                        pe.wait_ge(s_rsl, FT * n + k - 2 * FT + 1)
                    for wp, xp in PASSES:
                        if k < 2 * FT:
                            rhs = pq[:, slot, k, xp, :]
                        elif gi < 2 * FT:
                            rhs = split_t[:, xp, k - 2 * FT, cols(c)]
                        else:
                            rhs = rs16[:, xp, k - 2 * FT, :]
                        last = nc.tensor.matmul(dst[:, :], w16[:, k, wp, feat(gi)], rhs,
                                                start=i == 0 and (wp, xp) == PASSES[0],
                                                stop=i == KT - 1 and (wp, xp) == PASSES[-1])
                last.then_inc(s_gate, 1)

            def transposes(n, c, f):
                pe.wait_ge(s_sh, FT * n + f + 1)
                pe.wait_ge(s_sl, FT * n + f + 1)
                if not (isinstance(n, int) and n == 0 and f == 0):
                    pe.wait_ge(s_nat, 2 * n + f)
                for j in range(JC):
                    for part in range(2):
                        last = nc.tensor.transpose(tr16[:, j, part, :],
                                                   split_t[:, part, f, c * CW + j * P:c * CW + (j + 1) * P],
                                                   ident[:, :])
                last.then_inc(s_tr, 1)

            def head_hidden(c):
                n = CH * (STEPS - 1) + c
                for m in range(FT):
                    for k in range(FT):
                        if m == 0:
                            pe.wait_ge(s_sh, FT * n + k + 1)
                            pe.wait_ge(s_sl, FT * n + k + 1)
                        for wp, xp in PASSES:
                            last = nc.tensor.matmul(bank[4 + m][:, :], o16[:, k, wp, feat(m)],
                                                    split_t[:, xp, k, cols(c)],
                                                    start=k == 0 and (wp, xp) == PASSES[0],
                                                    stop=k == FT - 1 and (wp, xp) == PASSES[-1])
                    last.then_inc(s_o1, 1)

            def head_out(c):
                pe.wait_ge(s_hh, FT * (c + 1))
                pe.wait_ge(s_hl, FT * (c + 1))
                if c > 0:
                    pe.wait_ge(s_y, 2 * c)
                for j in range(JC):
                    for k in range(FT):
                        for wp, xp in PASSES:
                            last = nc.tensor.matmul(bank[6 + j // 2][:, (j % 2) * D:(j % 2 + 1) * D],
                                                    hid16[:, k, xp, j * P:(j + 1) * P], o16[:, k, wp, D:2 * D],
                                                    start=k == 0 and (wp, xp) == PASSES[0],
                                                    stop=k == FT - 1 and (wp, xp) == PASSES[-1])
                    if j % 2:
                        last.then_inc(s_o2, 1)

            def gates(n, c, slot, ready, last_step=False, between=None):
                for gi in range(GT):
                    if not (isinstance(n, int) and n == 0 and gi < 3):
                        pe.wait_ge(s_gfree, GT * n + gi - 2)
                    if last_step and c > 0 and gi < 2:
                        pe.wait_ge(s_hid, FT * (c - 1) + gi + 1)
                    if last_step and c > 0 and gi == 2:
                        pe.wait_ge(s_y, 2 * c - 1)
                    gate_tile(n, c, gi, slot, ready)
                    if between:
                        between(gi)

            def step(t, last):
                for c in range(CH):
                    n = CH * t + c
                    if c == 0:
                        pe.wait_ge(s_nat, 2 * n)
                        pe.nop(nofuse=True)
                    for q in range(2 * FT):
                        products(n, c, q, range(JH if c == 0 else 0, JT))
                        if c > 0 and not last and q < FT:
                            transposes(n - 1, c - 1, q)
                        if c > 0 and last and q == 0:
                            head_hidden(c - 1)
                        if c > 0 and last and q == 2:
                            head_out(c - 1)

                    def ready(k):
                        pe.wait_ge(s_pqh, 4 * (n - CH) + k + 1)
                        pe.wait_ge(s_pql, 4 * (n - CH) + k + 1)

                    gates(n, c, 0, ready, last_step=last)
                if not last:
                    pe.wait_ge(s_cur, t)
                    pe.nop(nofuse=True)
                    start_step(n)

            def start_step(n):
                for q in range(2 * FT):
                    products(n + 1, 0, q, range(0, JH))
                    if q == 1:
                        for f in range(FT):
                            transposes(n, CH - 1, f)

            pe.wait_ge(s_wl, 5)
            pe.wait_ge(s_deg, 2 * CH)
            for c in range(CH):
                def ready(k):
                    if k < FT:
                        pe.wait_ge(s_p0h, 2 * c + k + 1)
                        pe.wait_ge(s_p0l, 2 * c + k + 1)

                def between(gi):
                    if c > 0 and gi in (2, 3):
                        transposes(c - 1, c - 1, gi - 2)

                gates(c, c, c, ready, between=between)
            pe.wait_ge(s_nat, 2 * (CH - 1))
            start_step(CH - 1)
            with pe.Fori(1, STEPS - 1) as t:
                step(t, False)
            step(STEPS - 1, True)
            head_hidden(CH - 1)
            head_out(CH - 1)


def kernel(x, adj, L0_gnn_in_W, L0_gnn_in_b, L0_gnn_out_W, L0_gnn_out_b, L0_gnn_r_W, L0_gnn_r_b, L0_gnn_z_W,
           L0_gnn_z_b, L0_gnn_h_W, L0_gnn_h_b, L0_gnn_o1_W, L0_gnn_o1_b, L0_gnn_o2_W, L0_gnn_o2_b):
    import numpy as np
    import concourse.bacc as bacc
    from concourse.bass_utils import run_bass_kernel_spmd

    x, adj = np.asarray(x), np.asarray(adj)
    gates = [np.asarray(w) for w in (L0_gnn_r_W, L0_gnn_z_W, L0_gnn_h_W)]
    biases = (L0_gnn_in_b, L0_gnn_out_b, L0_gnn_r_b, L0_gnn_z_b, L0_gnn_h_b, L0_gnn_o1_b)
    arrays = {
        "x": x,
        "x_t": x.T,
        "adj": adj,
        "adj_t": adj.T,
        "io_w": np.concatenate([np.asarray(L0_gnn_in_W), np.asarray(L0_gnn_out_W)], axis=0),
        "gate_w": np.concatenate([w.T for w in gates], axis=1),
        "o_w": np.concatenate([np.asarray(L0_gnn_o1_W).T, np.asarray(L0_gnn_o2_W).T], axis=1),
        "bias": np.concatenate([np.asarray(b).reshape(FT, P).T for b in biases], axis=1),
        "o2_b": np.asarray(L0_gnn_o2_b),
    }
    arrays = {name: np.ascontiguousarray(a) for name, a in arrays.items()}
    nc = bacc.Bacc("TRN2", target_bir_lowering=False, num_devices=1)
    args = [nc.dram_tensor(f"in_{name}", a.shape, mybir.dt.from_np(a.dtype), kind="ExternalInput").ap()
            for name, a in arrays.items()]
    out = nc.dram_tensor("out", (N, D), F32, kind="ExternalOutput").ap()
    gnn_program(nc, *args, out)
    r = run_bass_kernel_spmd(nc, [{f"in_{name}": a for name, a in arrays.items()}], core_ids=[0])
    return r.results[0]["out"]
```

```python
import concourse.bass as bass
from concourse import mybir
from contextlib import ExitStack

F32 = mybir.dt.float32
F16 = mybir.dt.float16
F8 = mybir.dt.float8e4
I32 = mybir.dt.int32
U32 = mybir.dt.uint32
ACT = mybir.ActivationFunctionType
ALU = mybir.AluOpType
AX = mybir.AxisListType.X
RMAX = bass.bass_isa.ReduceOp.max

P = 128
N = 2048
D = 256
STEPS = 5
FT = D // P
JT = N // P
CW = 512
CH = N // CW
JC = CW // P
KT = 3 * FT
GD = 3 * D
GT = GD // P
STG = 3
JH = JT - JC

TOP = 2.0 ** 14
PSC = 1.0 / N
EXP_BITS = 0x7F800000
LN_EPS = 1e-5
NEWTON = 3
PASSES = ((0, 0), (0, 1), (1, 0))


def gnn_program(nc, x, x_t, adj, adj_t, io_w, gate_w, o_w, bias, o2_b, out):
    ctx = ExitStack()
    with ctx:
        def sb(name, shape, dt):
            return ctx.enter_context(nc.sbuf_tensor(name, shape, dt))

        def sem(name):
            return ctx.enter_context(nc.semaphore(name))

        a8 = sb("a8", [P, JT, N], F8)
        at_words = sb("at_words", [P, JT * N // 4], F32)
        at8 = at_words[:, :].bitcast(F8).rearrange("p (j n) -> p j n", j=JT)
        x_nat = at_words[:, JT * N // 8:].rearrange("p (j f) -> p j f", f=D)
        state_n = sb("state_n", [P, JT, 2, D], F16)
        state_t = sb("state_t", [P, FT, N], F32)
        split_t = sb("split_t", [P, 2, FT, N], F16)
        w16 = sb("w16", [P, KT, 2, GD], F16)
        o16 = sb("o16", [P, FT, 2, 2 * D], F16)

        pq_words = sb("pq_words", [P, CH * 2 * FT * CW], F32)
        pq = pq_words[:, :].bitcast(F16).rearrange("p (c q s n) -> p c q s n", c=CH, q=2 * FT, s=2)
        slot_words = 2 * FT * CW
        gw = pq_words[:, 0:KT * GD].rearrange("p (k m) -> p k m", k=KT)
        fold = pq_words[:, KT * GD:KT * GD + 2 * FT * GD].rearrange("p (k m) -> p k m", k=2 * FT)
        next_n = pq_words[:, slot_words:slot_words + JH * D].bitcast(F16) \
            .rearrange("p (j s f) -> p j s f", j=JH, s=2)
        y = pq_words[:, 3 * slot_words:4 * slot_words].rearrange("p (b j f) -> p b j f", b=2, j=JC)
        hid = pq_words[:, slot_words:slot_words + FT * CW].rearrange("p (k n) -> p k n", k=FT)
        hid16 = pq_words[:, slot_words + FT * CW:slot_words + 2 * FT * CW].bitcast(F16) \
            .rearrange("p (k s n) -> p k s n", k=FT, s=2)

        deg_words = sb("deg_words", [P, 2 * N // 2], F32)
        deg = deg_words[:, :].bitcast(F16).rearrange("p (d n) -> p d n", d=2)
        iow = deg_words[:, 0:2 * FT * D].rearrange("p (k m) -> p k m", k=2 * FT)
        ow = deg_words[:, 2 * FT * D:].rearrange("p (k m) -> p k m", k=FT)
        diag_words = sb("diag_words", [P, 2 * JT * P // 2], F32)
        diag = diag_words[:, :].bitcast(F16).rearrange("p (d j m) -> p d j m", d=2, j=JT)
        b2_all = diag_words[:, 0:D]

        tmp = sb("tmp", [P, STG * N], F32)
        stage = tmp[:, :].bitcast(I32).rearrange("p (s n) -> p s n", s=STG)
        pre = tmp[:, 0:3 * CW].rearrange("p (b n) -> p b n", b=3)
        r_buf = tmp[:, 3 * CW:5 * CW].rearrange("p (f n) -> p f n", f=FT)
        z_buf = tmp[:, 5 * CW:7 * CW].rearrange("p (f n) -> p f n", f=FT)
        h_buf = tmp[:, 7 * CW:9 * CW].rearrange("p (f n) -> p f n", f=FT)
        rs16 = tmp[:, 9 * CW:11 * CW].bitcast(F16).rearrange("p (s f n) -> p s f n", s=2, f=FT)

        ident = sb("ident", [P, P], F16)
        ones = sb("ones", [P, P], F16)
        bias_sb = sb("bias_sb", [P, 12], F32)
        degc = sb("degc", [P, 2, JT], F32)
        vdeg = sb("vdeg", [P, 2, GT], F32)
        mx = sb("mx", [P, 12], F32)
        mall = sb("mall", [P, 6], F32)
        scal = sb("scal", [P, 12], F32)
        ln_st = sb("ln_st", [P, JC, 6], F32)
        ln_mv = sb("ln_mv", [P, JC, 2], F32)
        ln_t = sb("ln_t", [P, 4, JC], F32)

        PX, SIG, PW, OMG, OMGP, UG, UO1, UO2, OM1, OM2, T0, T1 = [scal[:, i:i + 1] for i in range(12)]

        bank = [ctx.enter_context(nc.psum_tensor(f"bank{i}", [P, CW], F32)) for i in range(8)]
        gate_bank = bank[4:7]
        tr_bank = bank[7]
        tr16 = tr_bank[:, :].bitcast(F16).rearrange("p (j s f) -> p j s f", j=JC, s=2)

        s_iow, s_gws, s_ow, s_bias, s_b2 = [sem(n) for n in ("s_iow", "s_gws", "s_ow", "s_bias", "s_b2")]
        s_gwp = [sem("s_gwp0"), sem("s_gwp1")]
        s_xt = [sem("s_xt0"), sem("s_xt1")]
        s_x = [sem(f"s_x{c}") for c in range(CH)]
        s_adj = [sem(f"s_adj{i}") for i in range(STG)]
        s_cast = sem("s_cast")
        s_const0, s_const = sem("s_const0"), sem("s_const")
        s_mx, s_mall = sem("s_mx"), sem("s_mall")
        s_sc = sem("s_sc")
        s_snh, s_snl = sem("s_snh"), sem("s_snl")
        s_vdeg = sem("s_vdeg")
        s_fold, s_fev = sem("s_fold"), sem("s_fev")
        s_wh, s_wl = sem("s_wh"), sem("s_wl")
        s_q0, s_q0h, s_q0l = sem("s_q0"), sem("s_q0h"), sem("s_q0l")
        s_p0, s_p0h, s_p0l = sem("s_p0"), sem("s_p0h"), sem("s_p0l")
        s_diag, s_dg, s_deg = sem("s_diag"), sem("s_dg"), sem("s_deg")
        s_pq, s_pqh, s_pql = sem("s_pq"), sem("s_pqh"), sem("s_pql")
        s_gate = sem("s_gate")
        s_gfree = sem("s_gfree")
        s_pre = sem("s_pre")
        s_act = sem("s_act")
        s_rs, s_rsh, s_rsl = sem("s_rs"), sem("s_rsh"), sem("s_rsl")
        s_d, s_zd, s_new = sem("s_d"), sem("s_zd"), sem("s_new")
        s_sh, s_sl = sem("s_sh"), sem("s_sl")
        s_tr, s_nat = sem("s_tr"), sem("s_nat")
        s_cur = sem("s_cur")
        s_o1, s_hid, s_hh, s_hl = sem("s_o1"), sem("s_hid"), sem("s_hh"), sem("s_hl")
        s_o2, s_y, s_ln, s_norm = sem("s_o2"), sem("s_y"), sem("s_ln"), sem("s_norm")
        s_xr = [sem("s_xr0"), sem("s_xr1")]
        s_xb = sem("s_xb")
        s_out = [sem("s_out0"), sem("s_out1")]

        def cols(c):
            return slice(c * CW, (c + 1) * CW)

        def feat(f):
            return slice(f * P, (f + 1) * P)

        def p0_bank(c, f):
            return (2 * FT + 2 * c + f) % 8

        def store_rows(sp, c):
            for h in range(2):
                sp.wait_ge(s_norm, JC * c + 2 * h + 2)
                sp.dma_start(out.rearrange("(j p) f -> p j f", p=P)[:, c * JC + 2 * h:c * JC + 2 * h + 2, :],
                             y[:, c % 2, 2 * h:2 * h + 2, :]).then_inc(s_out[c % 2], 16)

        block = ctx.enter_context(nc.Block())

        @block.sync
        def _(sp):
            io_v = io_w.rearrange("(k p) m -> p k m", p=P)
            gw_v = gate_w.rearrange("(k p) m -> p k m", p=P)
            x_v = x.rearrange("(j p) f -> p j f", p=P)
            sp.dma_start(bias_sb[:, :], bias).then_inc(s_bias, 16)
            for d in range(2):
                sp.dma_start(gw[:, FT * d:FT * (d + 1), :], gw_v[:, FT * d:FT * (d + 1), :]).then_inc(s_gwp[d], 16)
                if d == 0:
                    sp.dma_start(iow, io_v).then_inc(s_iow, 16)
            for c in range(CH):
                sp.dma_start(x_nat[:, c * JC:(c + 1) * JC, :], x_v[:, c * JC:(c + 1) * JC, :]) \
                    .then_inc(s_x[c], 16)

            def load_rows(k):
                src = adj if k < JT else adj_t
                if k >= STG:
                    sp.wait_ge(s_cast, k - STG + 1)
                sp.dma_start(stage[:, k % STG, :], src[(k % JT) * P:(k % JT + 1) * P, :]) \
                    .then_inc(s_adj[k % STG], 16)

            for k in range(2 * JT):
                load_rows(k)
                if k == JC:
                    sp.dma_start(gw[:, 2 * FT:, :], gw_v[:, 2 * FT:, :]).then_inc(s_gws, 16)
                    sp.dma_start(ow, o_w.rearrange("(k p) m -> p k m", p=P)).then_inc(s_ow, 16)
                if k in (JT, JT + JC):
                    f = (k - JT) // JC
                    sp.dma_start(state_t[:, f, :], x_t[f * P:(f + 1) * P, :]).then_inc(s_xt[f], 16)

            sp.wait_ge(s_dg, 8)
            sp.dma_start(b2_all, o2_b.partition_broadcast(P)).then_inc(s_b2, 16)
            sp.wait_ge(s_gate, GT * CH)
            for c in range(CH):
                if c >= 2:
                    sp.wait_ge(s_out[c % 2], 32)
                sp.dma_start(y[:, c % 2, :, :], x_v[:, c * JC:(c + 1) * JC, :]).then_inc(s_xr[c % 2], 16)
                if c >= 1:
                    store_rows(sp, c - 1)
            store_rows(sp, CH - 1)
            sp.wait_ge(s_out[0], 16 * CH)
            sp.wait_ge(s_out[1], 16 * CH)

        @block.gpsimd
        def _(pool):
            nc.gpsimd.memset(ident[:, :], 0.0).then_inc(s_const0, 1)
            nc.gpsimd.memset(ones[:, :], 1.0).then_inc(s_const, 1)
            pool.wait_ge(s_const0, 1)
            nc.gpsimd.affine_select(out=ident[:, :], in_=ident[:, :], compare_op=ALU.not_equal, fill=1.0, base=0,
                                    pattern=[[-1, P]], channel_multiplier=1).then_inc(s_const, 1)
            pool.wait_ge(s_mx, 1)
            nc.gpsimd.partition_all_reduce(mall[:, 0:1], mx[:, 0:1], P, RMAX).then_inc(s_mall, 1)
            pool.wait_ge(s_mx, 2)
            nc.gpsimd.partition_all_reduce(mall[:, 1:5], mx[:, 1:5], P, RMAX).then_inc(s_mall, 1)
            pool.wait_ge(s_b2, 16)
            for c in range(CH):
                pool.wait_ge(s_xr[c % 2], 16 * (c // 2 + 1))
                for j in range(JC):
                    last = nc.gpsimd.tensor_tensor(y[:, c % 2, j, :], y[:, c % 2, j, :], b2_all, ALU.add)
                last.then_inc(s_xb, 1)

        @block.scalar
        def _(act):
            def fold_out(d):
                act.wait_ge(s_fold, d + 1)
                for k in range(FT):
                    nc.scalar.copy(fold[:, FT * d + k, 0:CW], bank[FT * d + k][:, :])
                    last = nc.scalar.copy(fold[:, FT * d + k, CW:GD], bank[4 + d][:, k * D:(k + 1) * D])
                last.then_inc(s_fev, 1)

            def cast_rows(k):
                act.wait_ge(s_adj[k % STG], 16 * (k // STG + 1))
                if k == JT + JT // 2:
                    act.wait_ge(s_snl, JT)
                dst = a8 if k < JT else at8
                nc.scalar.activation(dst[:, k % JT, :], stage[:, k % STG, :], ACT.Copy,
                                     accum_out=degc[:, k // JT, k % JT:k % JT + 1], saturate=False) \
                    .then_inc(s_cast, 1)

            fold_out(0)
            cast_rows(0)
            fold_out(1)
            act.wait_ge(s_vdeg, 1)
            nc.scalar.copy(vdeg[:, :, :], bank[6][:, 0:2 * GT].rearrange("p (d m) -> p d m", d=2)).then_inc(s_fev, 1)
            for k in range(1, JT):
                cast_rows(k)
            act.wait_ge(s_wl, 2)
            for c in range(CH):
                for f in range(FT):
                    act.wait_ge(s_q0, 2 * c + f + 1)
                    nc.scalar.activation(pq[:, c, FT + f, 0, :], bank[2 * c + f][:, :], ACT.Copy, scale=PSC) \
                        .then_inc(s_q0h, 1)
                cast_rows(JT + c)
            for k in range(JT + CH, 2 * JT):
                cast_rows(k)
            for c in range(CH):
                for f in range(FT):
                    act.wait_ge(s_p0, 2 * c + f + 1)
                    nc.scalar.activation(pq[:, c, f, 0, :], bank[p0_bank(c, f)][:, :], ACT.Copy, scale=PSC) \
                        .then_inc(s_p0h, 1)

            def pq_hi(n, q):
                act.wait_ge(s_pq, 4 * (n - CH) + q + 1)
                nc.scalar.activation(pq[:, 0, q, 0, :], bank[q][:, :], ACT.Copy, scale=PSC).then_inc(s_pqh, 1)

            def nat_out(n, c, f, direct):
                dst = state_n if direct or c == CH - 1 else next_n
                act.wait_ge(s_tr, 2 * n + f + 1)
                nc.scalar.copy(dst[:, c * JC:(c + 1) * JC, :, feat(f)], tr16).then_inc(s_nat, 1)

            def gate_act(n, gi):
                dst = (r_buf, z_buf, h_buf)[gi // FT]
                act.wait_ge(s_pre, GT * n + gi + 1)
                nc.scalar.activation(dst[:, gi % FT, :], pre[:, gi % 3, :], ACT.Tanh if gi >= 2 * FT else ACT.Sigmoid,
                                     bias=bias_sb[:, 4 + gi:5 + gi], scale=UG).then_inc(s_act, 1)

            def gates(n, c, between=False):
                gate_act(n, 0)
                gate_act(n, 1)
                for f in range(FT):
                    act.wait_ge(s_rs, FT * n + f + 1)
                    nc.scalar.activation(rs16[:, 0, f, :], r_buf[:, f, :], ACT.Copy, scale=SIG).then_inc(s_rsh, 1)
                for f in range(FT):
                    gate_act(n, 2 + f)
                    if between:
                        nat_out(n - 1, c - 1, f, True)
                for f in range(FT):
                    gate_act(n, 4 + f)
                    act.wait_ge(s_new, FT * n + f + 1)
                    nc.scalar.activation(split_t[:, 0, f, cols(c)], state_t[:, f, cols(c)], ACT.Copy, scale=SIG) \
                        .then_inc(s_sh, 1)

            def head_act(c):
                for m in range(FT):
                    act.wait_ge(s_o1, FT * c + m + 1)
                    nc.scalar.activation(hid[:, m, :], bank[4 + m][:, :], ACT.Tanh,
                                         bias=bias_sb[:, 10 + m:11 + m], scale=UO1).then_inc(s_hid, 1)
                for m in range(FT):
                    act.wait_ge(s_hid, FT * c + m + 1)
                    nc.scalar.activation(hid16[:, m, 0, :], hid[:, m, :], ACT.Copy, scale=TOP).then_inc(s_hh, 1)

            def step(t, last, first_direct):
                for c in range(CH):
                    n = CH * t + c
                    if c == 0:
                        nat_out(n - 1, CH - 1, 0, first_direct)
                        nat_out(n - 1, CH - 1, 1, first_direct)
                    pq_hi(n, 0)
                    if c > 0 and not last:
                        nat_out(n - 1, c - 1, 0, False)
                    if c > 0 and last:
                        head_act(c - 1)
                    pq_hi(n, 1)
                    if c > 0 and not last:
                        nat_out(n - 1, c - 1, 1, False)
                    pq_hi(n, 2)
                    pq_hi(n, 3)
                    gates(n, c)
                if last:
                    head_act(CH - 1)

            for c in range(CH):
                gates(c, c, between=c > 0)
            with act.Fori(1, STEPS - 1) as t:
                step(t, False, True)
            step(STEPS - 1, True, True)

        @block.vector
        def _(dve):
            chain = [0]

            def link(ins):
                chain[0] += 1
                ins.then_inc(s_sc, 1)
                dve.wait_ge(s_sc, chain[0])

            for c in range(CH):
                dve.wait_ge(s_x[c], 16)
                last = nc.vector.tensor_reduce(mx[:, 8 + c:9 + c], x_nat[:, c * JC:(c + 1) * JC, :],
                                               mybir.AxisListType.XY, ALU.max, apply_absolute_value=True)
            link(last)
            nc.vector.tensor_reduce(mx[:, 0:1], mx[:, 8:12], AX, ALU.max).then_inc(s_mx, 1)
            dve.wait_ge(s_mall, 1)
            link(nc.vector.tensor_scalar(T0, mall[:, 0:1], 1.0, None, ALU.max))
            link(nc.vector.tensor_scalar(PX.bitcast(U32), T0.bitcast(U32), EXP_BITS, None, ALU.bitwise_and))
            link(nc.vector.reciprocal(T1, PX))
            link(nc.vector.tensor_scalar(SIG, T1, TOP, None, ALU.mult))
            for c in range(CH):
                nc.vector.tensor_scalar(state_n[:, c * JC:(c + 1) * JC, 0, :], x_nat[:, c * JC:(c + 1) * JC, :], SIG,
                                        None, ALU.mult).then_inc(s_snh, 1)
                dve.wait_ge(s_snh, c + 1)
                for j in range(c * JC, (c + 1) * JC):
                    nc.vector.scalar_tensor_tensor(state_n[:, j, 1, :], x_nat[:, j, :], SIG, state_n[:, j, 0, :],
                                                   ALU.mult, ALU.subtract).then_inc(s_snl, 1)
            dve.wait_ge(s_fev, 2)
            nc.vector.tensor_reduce(mx[:, 1:2], fold, mybir.AxisListType.XY, ALU.max, apply_absolute_value=True)
            dve.wait_ge(s_gws, 16)
            nc.vector.tensor_reduce(mx[:, 2:3], gw[:, 2 * FT:, :], mybir.AxisListType.XY, ALU.max,
                                    apply_absolute_value=True)
            dve.wait_ge(s_ow, 16)
            nc.vector.tensor_reduce(mx[:, 3:4], ow[:, :, 0:D], mybir.AxisListType.XY, ALU.max,
                                    apply_absolute_value=True)
            nc.vector.tensor_reduce(mx[:, 4:5], ow[:, :, D:2 * D], mybir.AxisListType.XY, ALU.max,
                                    apply_absolute_value=True).then_inc(s_mx, 1)
            dve.wait_ge(s_mall, 2)
            link(nc.vector.tensor_scalar(T0, mall[:, 1:2], 1.0 / PSC, 1e-30, ALU.mult, ALU.max))
            link(nc.vector.tensor_tensor(T1, T0, mall[:, 2:3], ALU.max))
            link(nc.vector.tensor_scalar(PW.bitcast(U32), T1.bitcast(U32), EXP_BITS, None, ALU.bitwise_and))
            link(nc.vector.reciprocal(T0, PW))
            link(nc.vector.tensor_scalar(OMG, T0, TOP, None, ALU.mult))
            link(nc.vector.tensor_scalar(OMGP, T0, TOP / PSC, None, ALU.mult))
            link(nc.vector.tensor_scalar(UG, PW, PX, 1.0 / (TOP * TOP), ALU.mult, ALU.mult))
            for src, om, un in ((mall[:, 3:4], OM1, UO1), (mall[:, 4:5], OM2, UO2)):
                link(nc.vector.tensor_scalar(T0, src, 1e-30, None, ALU.max))
                link(nc.vector.tensor_scalar(un.bitcast(U32), T0.bitcast(U32), EXP_BITS, None, ALU.bitwise_and))
                link(nc.vector.reciprocal(T1, un))
                link(nc.vector.tensor_scalar(om, T1, TOP, None, ALU.mult))
            link(nc.vector.tensor_scalar(T0, UO1, PX, 1.0 / (TOP * TOP), ALU.mult, ALU.mult))
            link(nc.vector.tensor_copy(UO1, T0))
            link(nc.vector.tensor_scalar(T1, UO2, 1.0 / (TOP * TOP), None, ALU.mult))
            link(nc.vector.tensor_copy(UO2, T1))
            dve.wait_ge(s_fev, 3)
            link(nc.vector.tensor_scalar(vdeg[:, :, :], vdeg[:, :, :], SIG, OMG, ALU.mult, ALU.mult))
            parts = ((w16[:, 0:2 * FT, :, :], fold, OMGP), (w16[:, 2 * FT:, :, :], gw[:, 2 * FT:, :], OMG),
                     (o16[:, :, :, 0:D], ow[:, :, 0:D], OM1), (o16[:, :, :, D:2 * D], ow[:, :, D:2 * D], OM2))
            for i, (dst, src, om) in enumerate(parts):
                nc.vector.tensor_scalar(dst[:, :, 0, :], src, om, None, ALU.mult).then_inc(s_wh, 1)
                dve.wait_ge(s_wh, i + 1)
                nc.vector.scalar_tensor_tensor(dst[:, :, 1, :], src, om, dst[:, :, 0, :], ALU.mult, ALU.subtract) \
                    .then_inc(s_wl, 1)
            def split_first(f):
                dve.wait_ge(s_xt[f], 16)
                nc.vector.tensor_scalar(split_t[:, 0, f, :], state_t[:, f, :], SIG, None, ALU.mult).then_inc(s_wh, 1)
                dve.wait_ge(s_wh, 5 + f)
                nc.vector.scalar_tensor_tensor(split_t[:, 1, f, :], state_t[:, f, :], SIG, split_t[:, 0, f, :],
                                               ALU.mult, ALU.subtract).then_inc(s_wl, 1)

            def lo_of_psum(c, q, src, done):
                return nc.vector.scalar_tensor_tensor(pq[:, c, q, 1, :], src[:, :], PSC, pq[:, c, q, 0, :],
                                                      ALU.mult, ALU.subtract).then_inc(done, 1)

            dve.wait_ge(s_const, 2)

            def make_diag(d):
                dve.wait_ge(s_cast, JT * (d + 1))
                for j in range(JT):
                    last = nc.vector.tensor_scalar(diag[:, d, j, :], ident[:, :], degc[:, d, j:j + 1], None, ALU.mult)
                last.then_inc(s_diag, 1)

            make_diag(0)
            for c in range(CH):
                for f in range(FT):
                    dve.wait_ge(s_q0h, 2 * c + f + 1)
                    lo_of_psum(c, FT + f, bank[2 * c + f], s_q0l)
            split_first(0)
            split_first(1)
            make_diag(1)

            def p0_lo(c, f):
                dve.wait_ge(s_p0h, 2 * c + f + 1)
                lo_of_psum(c, f, bank[p0_bank(c, f)], s_p0l)

            def deg_out(d):
                for c in range(CH):
                    dve.wait_ge(s_dg, CH * d + c + 1)
                    nc.vector.tensor_copy(deg[:, d, cols(c)], bank[4 + c][:, :]).then_inc(s_deg, 1)

            for c in range(CH):
                p0_lo(c, 0)
                if c >= CH - 2:
                    deg_out(c - (CH - 2))
                p0_lo(c, 1)
            dve.wait_ge(s_deg, 2 * CH)

            def gate_pre(n, c, gi):
                g = GT * n + gi
                dve.wait_ge(s_gate, g + 1)
                if not (isinstance(n, int) and n == 0 and gi < 3):
                    dve.wait_ge(s_act, g - 2)
                nc.vector.scalar_tensor_tensor(pre[:, gi % 3, :], deg[:, 0, cols(c)], vdeg[:, 0, gi:gi + 1],
                                               gate_bank[gi % 3][:, :], ALU.mult, ALU.add).then_inc(s_gfree, 1)
                dve.wait_ge(s_gfree, g + 1)
                nc.vector.scalar_tensor_tensor(pre[:, gi % 3, :], deg[:, 1, cols(c)], vdeg[:, 1, gi:gi + 1],
                                               pre[:, gi % 3, :], ALU.mult, ALU.add).then_inc(s_pre, 1)

            def reset_part(n, c):
                for f in range(FT):
                    dve.wait_ge(s_act, GT * n + f + 1)
                    nc.vector.tensor_tensor(r_buf[:, f, :], r_buf[:, f, :], state_t[:, f, cols(c)], ALU.mult) \
                        .then_inc(s_rs, 1)
                for f in range(FT):
                    dve.wait_ge(s_rsh, FT * n + f + 1)
                    nc.vector.scalar_tensor_tensor(rs16[:, 1, f, :], r_buf[:, f, :], SIG, rs16[:, 0, f, :],
                                                   ALU.mult, ALU.subtract).then_inc(s_rsl, 1)

            def update(n, c, f):
                k = FT * n + f + 1
                dve.wait_ge(s_act, GT * n + 4 + f + 1)
                nc.vector.tensor_tensor(h_buf[:, f, :], h_buf[:, f, :], state_t[:, f, cols(c)], ALU.subtract) \
                    .then_inc(s_d, 1)
                dve.wait_ge(s_d, k)
                nc.vector.tensor_tensor(z_buf[:, f, :], z_buf[:, f, :], h_buf[:, f, :], ALU.mult).then_inc(s_zd, 1)
                dve.wait_ge(s_zd, k)
                nc.vector.tensor_tensor(state_t[:, f, cols(c)], state_t[:, f, cols(c)], z_buf[:, f, :], ALU.add) \
                    .then_inc(s_new, 1)

            def update_lo(n, c, f):
                k = FT * n + f + 1
                dve.wait_ge(s_sh, k)
                nc.vector.scalar_tensor_tensor(split_t[:, 1, f, cols(c)], state_t[:, f, cols(c)], SIG,
                                               split_t[:, 0, f, cols(c)], ALU.mult, ALU.subtract) \
                    .then_inc(s_sl, 1)

            def gates(n, c):
                gate_pre(n, c, 0)
                gate_pre(n, c, 1)
                reset_part(n, c)
                gate_pre(n, c, 2)
                gate_pre(n, c, 3)
                gate_pre(n, c, 4)
                update(n, c, 0)
                gate_pre(n, c, 5)
                update_lo(n, c, 0)
                update(n, c, 1)
                update_lo(n, c, 1)

            def head_lo(c):
                for m in range(FT):
                    dve.wait_ge(s_hh, FT * c + m + 1)
                    nc.vector.scalar_tensor_tensor(hid16[:, m, 1, :], hid[:, m, :], TOP, hid16[:, m, 0, :],
                                                   ALU.mult, ALU.subtract).then_inc(s_hl, 1)

            def residual(c, h):
                dve.wait_ge(s_xb, c + 1)
                dve.wait_ge(s_o2, 2 * c + h + 1)
                rows = y[:, c % 2, 2 * h:2 * h + 2, :]
                nc.vector.scalar_tensor_tensor(rows, bank[6 + h][:, :].rearrange("p (j f) -> p j f", j=2), UO2,
                                               rows, ALU.mult, ALU.add).then_inc(s_y, 1)

            ln_chain = [0]

            def ln_link(ins):
                ln_chain[0] += 1
                ins.then_inc(s_ln, 1)
                dve.wait_ge(s_ln, ln_chain[0])

            def layer_norm(c, h):
                js = slice(2 * h, 2 * h + 2)
                dve.wait_ge(s_y, 2 * c + h + 1)
                for j in (2 * h, 2 * h + 1):
                    last = nc.vector.bn_stats(ln_st[:, j, :], y[:, c % 2, j, :])
                ln_link(last)
                for j in (2 * h, 2 * h + 1):
                    last = nc.vector.bn_aggr(ln_mv[:, j, :], ln_st[:, j, :])
                ln_link(last)
                var, a, b, r = [ln_t[:, i, js] for i in range(4)]
                ln_link(nc.vector.tensor_scalar(var, ln_mv[:, js, 1], LN_EPS, None, ALU.add))
                ln_link(nc.vector.tensor_scalar(a.bitcast(U32), var.bitcast(U32), 1, None, ALU.logical_shift_right))
                ln_link(nc.vector.tensor_scalar(r.bitcast(I32), a.bitcast(I32), -1.0, float(0x5F3759DF),
                                                ALU.mult, ALU.add))
                for _ in range(NEWTON):
                    ln_link(nc.vector.tensor_tensor(a, r, r, ALU.mult))
                    ln_link(nc.vector.scalar_tensor_tensor(b, a, -0.5, var, ALU.mult, ALU.mult))
                    ln_link(nc.vector.scalar_tensor_tensor(r, b, 1.5, r, ALU.add, ALU.mult))
                for j in (2 * h, 2 * h + 1):
                    nc.vector.tensor_scalar(y[:, c % 2, j, :], y[:, c % 2, j, :], ln_mv[:, j, 0:1], ln_t[:, 3, j:j + 1],
                                            ALU.subtract, ALU.mult).then_inc(s_norm, 1)

            def pq_lo(n, q):
                dve.wait_ge(s_pqh, 4 * (n - CH) + q + 1)
                lo_of_psum(0, q, bank[q], s_pql)

            def step(t, last):
                for c in range(CH):
                    n = CH * t + c
                    pq_lo(n, 0)
                    if last and c > 0:
                        head_lo(c - 1)
                    pq_lo(n, 1)
                    pq_lo(n, 2)
                    if last and c > 0:
                        for h in range(2):
                            residual(c - 1, h)
                        for h in range(2):
                            layer_norm(c - 1, h)
                    pq_lo(n, 3)
                    if c == CH - 1 and not last:
                        dve.wait_ge(s_nat, 2 * n)
                        nc.vector.tensor_copy(state_n[:, 0:JH, :, :], next_n).then_inc(s_cur, 1)
                    gates(n, c)
                if last:
                    head_lo(CH - 1)
                    for h in range(2):
                        residual(CH - 1, h)
                        layer_norm(CH - 1, h)

            for c in range(CH):
                gates(c, c)
            with dve.Fori(1, STEPS - 1) as t:
                step(t, False)
            step(STEPS - 1, True)

        @block.tensor
        def _(pe):
            pe.wait_ge(s_iow, 16)
            for d in range(2):
                pe.wait_ge(s_gwp[d], 16)
                for k in range(FT):
                    o = FT * d + k
                    for dst, lo, hi in ((bank[o][:, :], 0, CW), (bank[4 + d][:, k * D:(k + 1) * D], CW, GD)):
                        for ct in range(FT):
                            last = nc.tensor.matmul(dst, iow[:, FT * d + ct, feat(k)], gw[:, FT * d + ct, lo:hi],
                                                    start=ct == 0, stop=ct == FT - 1)
                last.then_inc(s_fold, 1)
            pe.wait_ge(s_bias, 16)
            for d in range(2):
                for m in range(GT):
                    for ct in range(FT):
                        last = nc.tensor.matmul(bank[6][:, d * GT + m:d * GT + m + 1], gw[:, FT * d + ct, feat(m)],
                                                bias_sb[:, FT * d + ct:FT * d + ct + 1],
                                                start=ct == 0, stop=ct == FT - 1)
            last.then_inc(s_vdeg, 1)

            def adj_mm(dst, adj8, j, part, f, c):
                return nc.tensor.matmul(dst[:, :], state_n[:, j, part, feat(f)], adj8[:, j, cols(c)],
                                        start=j == 0 and part == 0, stop=j == JT - 1 and part == 1)

            pe.wait_ge(s_fev, 3)
            for j in range(JH):
                pe.wait_ge(s_snl, j + 1)
                pe.wait_ge(s_cast, j + 1)
                for f in range(FT):
                    for part in range(2):
                        for c in range(CH):
                            adj_mm(bank[2 * c + f], a8, j, part, f, c)
            pe.wait_ge(s_snl, JT)
            pe.wait_ge(s_cast, JT)
            for c in range(CH):
                for f in range(FT):
                    for j in range(JH, JT):
                        for part in range(2):
                            last = adj_mm(bank[2 * c + f], a8, j, part, f, c)
                    last.then_inc(s_q0, 1)
            for j in range(JH):
                pe.wait_ge(s_cast, JT + j + 1)
                for c in (2, 3, 0, 1):
                    for f in range(FT):
                        if j == 0:
                            pe.wait_ge(s_q0h, p0_bank(c, f) + 1)
                            pe.wait_ge(s_q0l, p0_bank(c, f) + 1)
                        for part in range(2):
                            adj_mm(bank[p0_bank(c, f)], at8, j, part, f, c)
            pe.wait_ge(s_cast, 2 * JT)

            def spread_degrees(d):
                pe.wait_ge(s_diag, d + 1)
                for c in range(CH):
                    if d == 0:
                        pe.wait_ge(s_p0h, c + 1)
                        pe.wait_ge(s_p0l, c + 1)
                    else:
                        pe.wait_ge(s_deg, c + 1)
                    nc.tensor.matmul(bank[4 + c][:, :], ones[:, :], diag[:, d, c * JC:(c + 1) * JC, :],
                                     start=True, stop=True).then_inc(s_dg, 1)

            pe.wait_ge(s_const, 2)
            for c in range(CH):
                for f in range(FT):
                    for j in range(JH, JT):
                        for part in range(2):
                            last = adj_mm(bank[p0_bank(c, f)], at8, j, part, f, c)
                    last.then_inc(s_p0, 1)
                    if c >= CH - 2 and f == 0:
                        spread_degrees(c - (CH - 2))

            def products(n, c, q, tiles):
                for j in tiles:
                    for part in range(2):
                        last = adj_mm(bank[q], (at8, a8)[q // FT], j, part, q % FT, c)
                if tiles[-1] == JT - 1:
                    last.then_inc(s_pq, 1)

            def gate_tile(n, c, gi, slot, ready):
                dst = gate_bank[gi % 3]
                adj_k = [0, 1, 2, 3]
                state_k = [4, 5]
                order = state_k + adj_k if gi < 2 * FT else adj_k + state_k
                for i, k in enumerate(order):
                    if k < 2 * FT and gi == 0:
                        ready(k)
                    if k >= 2 * FT and gi == 2 * FT:
                        pe.wait_ge(s_rsh, FT * n + k - 2 * FT + 1)
                        pe.wait_ge(s_rsl, FT * n + k - 2 * FT + 1)
                    for wp, xp in PASSES:
                        if k < 2 * FT:
                            rhs = pq[:, slot, k, xp, :]
                        elif gi < 2 * FT:
                            rhs = split_t[:, xp, k - 2 * FT, cols(c)]
                        else:
                            rhs = rs16[:, xp, k - 2 * FT, :]
                        last = nc.tensor.matmul(dst[:, :], w16[:, k, wp, feat(gi)], rhs,
                                                start=i == 0 and (wp, xp) == PASSES[0],
                                                stop=i == KT - 1 and (wp, xp) == PASSES[-1])
                last.then_inc(s_gate, 1)

            def transposes(n, c, f):
                pe.wait_ge(s_sh, FT * n + f + 1)
                pe.wait_ge(s_sl, FT * n + f + 1)
                if isinstance(n, int) and n == 0 and f == 0:
                    pe.wait_ge(s_deg, 2 * CH)
                else:
                    pe.wait_ge(s_nat, 2 * n + f)
                for j in range(JC):
                    for part in range(2):
                        last = nc.tensor.transpose(tr16[:, j, part, :],
                                                   split_t[:, part, f, c * CW + j * P:c * CW + (j + 1) * P],
                                                   ident[:, :])
                last.then_inc(s_tr, 1)

            def head_hidden(c):
                n = CH * (STEPS - 1) + c
                for k in range(FT):
                    pe.wait_ge(s_sh, FT * n + k + 1)
                    pe.wait_ge(s_sl, FT * n + k + 1)
                    for m in range(FT):
                        for wp, xp in PASSES:
                            last = nc.tensor.matmul(bank[4 + m][:, :], o16[:, k, wp, feat(m)],
                                                    split_t[:, xp, k, cols(c)],
                                                    start=k == 0 and (wp, xp) == PASSES[0],
                                                    stop=k == FT - 1 and (wp, xp) == PASSES[-1])
                        if k == FT - 1:
                            last.then_inc(s_o1, 1)

            def head_out(c):
                pe.wait_ge(s_hh, FT * (c + 1))
                pe.wait_ge(s_hl, FT * (c + 1))
                if c > 0:
                    pe.wait_ge(s_y, 2 * c)
                for j in range(JC):
                    for k in range(FT):
                        for wp, xp in PASSES:
                            last = nc.tensor.matmul(bank[6 + j // 2][:, (j % 2) * D:(j % 2 + 1) * D],
                                                    hid16[:, k, xp, j * P:(j + 1) * P], o16[:, k, wp, D:2 * D],
                                                    start=k == 0 and (wp, xp) == PASSES[0],
                                                    stop=k == FT - 1 and (wp, xp) == PASSES[-1])
                    if j % 2:
                        last.then_inc(s_o2, 1)

            def gates(n, c, slot, ready, last_step=False, between=None):
                for gi in range(GT):
                    if isinstance(n, int) and n == 0 and gi < 3:
                        pe.wait_ge(s_deg, CH + gi + 1)
                    else:
                        pe.wait_ge(s_gfree, GT * n + gi - 2)
                    if last_step and c > 0 and gi < 2:
                        pe.wait_ge(s_hid, FT * (c - 1) + gi + 1)
                    if last_step and c > 0 and gi == 2:
                        pe.wait_ge(s_y, 2 * c - 1)
                    gate_tile(n, c, gi, slot, ready)
                    if between:
                        between(gi)

            def step(t, last):
                for c in range(CH):
                    n = CH * t + c
                    if c == 0:
                        pe.wait_ge(s_nat, 2 * n)
                        pe.nop(nofuse=True)
                    for q in range(2 * FT):
                        products(n, c, q, range(JH if c == 0 else 0, JT))
                        if c > 0 and not last and q < FT:
                            transposes(n - 1, c - 1, q)
                        if c > 0 and last and q == 0:
                            head_hidden(c - 1)
                        if c > 0 and last and q == 2:
                            head_out(c - 1)

                    def ready(k):
                        pe.wait_ge(s_pqh, 4 * (n - CH) + k + 1)
                        pe.wait_ge(s_pql, 4 * (n - CH) + k + 1)

                    gates(n, c, 0, ready, last_step=last)
                if not last:
                    pe.wait_ge(s_cur, t)
                    pe.nop(nofuse=True)
                    start_step(n)

            def start_step(n):
                for q in range(2 * FT):
                    products(n + 1, 0, q, range(0, JH))
                    if q in (1, 2):
                        transposes(n, CH - 1, q - 1)

            pe.wait_ge(s_wl, 6)
            for c in range(CH):
                def ready(k):
                    if k < FT:
                        pe.wait_ge(s_p0h, 2 * c + k + 1)
                        pe.wait_ge(s_p0l, 2 * c + k + 1)

                def between(gi):
                    if c > 0 and gi in (2, 3):
                        transposes(c - 1, c - 1, gi - 2)

                gates(c, c, c, ready, between=between)
            pe.wait_ge(s_nat, 2 * (CH - 1))
            start_step(CH - 1)
            with pe.Fori(1, STEPS - 1) as t:
                step(t, False)
            step(STEPS - 1, True)
            head_hidden(CH - 1)
            head_out(CH - 1)


def kernel(x, adj, L0_gnn_in_W, L0_gnn_in_b, L0_gnn_out_W, L0_gnn_out_b, L0_gnn_r_W, L0_gnn_r_b, L0_gnn_z_W,
           L0_gnn_z_b, L0_gnn_h_W, L0_gnn_h_b, L0_gnn_o1_W, L0_gnn_o1_b, L0_gnn_o2_W, L0_gnn_o2_b):
    import numpy as np
    import concourse.bacc as bacc
    from concourse.bass_utils import run_bass_kernel_spmd

    x, adj = np.asarray(x), np.asarray(adj)
    gates = [np.asarray(w) for w in (L0_gnn_r_W, L0_gnn_z_W, L0_gnn_h_W)]
    biases = (L0_gnn_in_b, L0_gnn_out_b, L0_gnn_r_b, L0_gnn_z_b, L0_gnn_h_b, L0_gnn_o1_b)
    arrays = {
        "x": x,
        "x_t": x.T,
        "adj": adj,
        "adj_t": adj.T,
        "io_w": np.concatenate([np.asarray(L0_gnn_in_W), np.asarray(L0_gnn_out_W)], axis=0),
        "gate_w": np.concatenate([w.T for w in gates], axis=1),
        "o_w": np.concatenate([np.asarray(L0_gnn_o1_W).T, np.asarray(L0_gnn_o2_W).T], axis=1),
        "bias": np.concatenate([np.asarray(b).reshape(FT, P).T for b in biases], axis=1),
        "o2_b": np.asarray(L0_gnn_o2_b),
    }
    arrays = {name: np.ascontiguousarray(a) for name, a in arrays.items()}
    nc = bacc.Bacc("TRN2", target_bir_lowering=False, num_devices=1)
    args = [nc.dram_tensor(f"in_{name}", a.shape, mybir.dt.from_np(a.dtype), kind="ExternalInput").ap()
            for name, a in arrays.items()]
    out = nc.dram_tensor("out", (N, D), F32, kind="ExternalOutput").ap()
    gnn_program(nc, *args, out)
    r = run_bass_kernel_spmd(nc, [{f"in_{name}": a for name, a in arrays.items()}], core_ids=[0])
    return r.results[0]["out"]
```

```python
import concourse.bass as bass
from concourse import mybir
from contextlib import ExitStack

F32 = mybir.dt.float32
F16 = mybir.dt.float16
F8 = mybir.dt.float8e4
I32 = mybir.dt.int32
U32 = mybir.dt.uint32
ACT = mybir.ActivationFunctionType
ALU = mybir.AluOpType
AX = mybir.AxisListType.X
RMAX = bass.bass_isa.ReduceOp.max
RADD = bass.bass_isa.ReduceOp.add

P = 128
N = 2048
D = 256
STEPS = 5
FT = D // P
JT = N // P
CW = 512
CH = N // CW
JC = CW // P
KT = 3 * FT
GD = 3 * D
GT = GD // P
STG = 3
JH = JT - JC
JQ = JT - 2

TOP = 2.0 ** 14
PSC = 1.0 / N
EXP_BITS = 0x7F800000
LN_EPS = 1e-5
NEWTON = 3
PASSES = ((0, 0), (0, 1), (1, 0))


def gnn_program(nc, x, x_t, adj, adj_t, io_w, gate_w, o_w, bias, o2_b, out):
    ctx = ExitStack()
    with ctx:
        def sb(name, shape, dt):
            return ctx.enter_context(nc.sbuf_tensor(name, shape, dt))

        def sem(name):
            return ctx.enter_context(nc.semaphore(name))

        a8 = sb("a8", [P, JT, N], F8)
        at_words = sb("at_words", [P, JT * N // 4], F32)
        at8 = at_words[:, :].bitcast(F8).rearrange("p (j n) -> p j n", j=JT)
        x_nat = at_words[:, JT * N // 8:].rearrange("p (j f) -> p j f", f=D)
        x_words = at_words[:, JT * N // 8:]
        v_part = x_words[:, 0:2 * GD].rearrange("p (d m) -> p d m", d=2)
        v_sum = x_words[:, 2 * GD:4 * GD].rearrange("p (d m) -> p d m", d=2)
        state_n = sb("state_n", [P, JT, 2, D], F16)
        state_t = sb("state_t", [P, FT, N], F32)
        split_t = sb("split_t", [P, 2, FT, N], F16)
        w16 = sb("w16", [P, KT, 2, GD], F16)
        o16 = sb("o16", [P, FT, 2, 2 * D], F16)

        pq_words = sb("pq_words", [P, CH * 2 * FT * CW], F32)
        pq = pq_words[:, :].bitcast(F16).rearrange("p (c q s n) -> p c q s n", c=CH, q=2 * FT, s=2)
        slot_words = 2 * FT * CW
        gw = pq_words[:, 0:KT * GD].rearrange("p (k m) -> p k m", k=KT)
        fold = pq_words[:, KT * GD:KT * GD + 2 * FT * GD].rearrange("p (k m) -> p k m", k=2 * FT)
        next_n = pq_words[:, slot_words:slot_words + JH * D].bitcast(F16) \
            .rearrange("p (j s f) -> p j s f", j=JH, s=2)
        y = pq_words[:, 3 * slot_words:4 * slot_words].rearrange("p (b j f) -> p b j f", b=2, j=JC)
        hid = pq_words[:, slot_words:slot_words + FT * CW].rearrange("p (k n) -> p k n", k=FT)
        hid16 = pq_words[:, slot_words + FT * CW:slot_words + 2 * FT * CW].bitcast(F16) \
            .rearrange("p (k s n) -> p k s n", k=FT, s=2)

        deg_words = sb("deg_words", [P, 2 * N // 2], F32)
        deg = deg_words[:, :].bitcast(F16).rearrange("p (d n) -> p d n", d=2)
        iow = deg_words[:, 0:2 * FT * D].rearrange("p (k m) -> p k m", k=2 * FT)
        ow = deg_words[:, 2 * FT * D:].rearrange("p (k m) -> p k m", k=FT)
        diag_words = sb("diag_words", [P, 2 * JT * P // 2], F32)
        diag = diag_words[:, :].bitcast(F16).rearrange("p (d j m) -> p d j m", d=2, j=JT)
        b2_all = diag_words[:, 0:D]

        tmp = sb("tmp", [P, STG * N], F32)
        stage = tmp[:, :].bitcast(I32).rearrange("p (s n) -> p s n", s=STG)
        pre = tmp[:, 0:3 * CW].rearrange("p (b n) -> p b n", b=3)
        r_buf = tmp[:, 3 * CW:5 * CW].rearrange("p (f n) -> p f n", f=FT)
        z_buf = tmp[:, 5 * CW:7 * CW].rearrange("p (f n) -> p f n", f=FT)
        h_buf = tmp[:, 7 * CW:9 * CW].rearrange("p (f n) -> p f n", f=FT)
        rs16 = tmp[:, 9 * CW:11 * CW].bitcast(F16).rearrange("p (s f n) -> p s f n", s=2, f=FT)

        ident = sb("ident", [P, P], F16)
        ones = sb("ones", [P, P], F16)
        bias_sb = sb("bias_sb", [P, 12], F32)
        degc = sb("degc", [P, 2, JT], F32)
        vdeg = sb("vdeg", [P, 2, GT], F32)
        mx = sb("mx", [P, 12], F32)
        mall = sb("mall", [P, 6], F32)
        scal = sb("scal", [P, 12], F32)
        ln_st = sb("ln_st", [P, JC, 6], F32)
        ln_mv = sb("ln_mv", [P, JC, 2], F32)
        ln_t = sb("ln_t", [P, 4, JC], F32)

        PX, SIG, PW, OMG, OMGP, UG, UO1, UO2, OM1, OM2, T0, T1 = [scal[:, i:i + 1] for i in range(12)]

        bank = [ctx.enter_context(nc.psum_tensor(f"bank{i}", [P, CW], F32)) for i in range(8)]
        gate_bank = bank[4:7]
        tr_bank = bank[7]
        tr16 = tr_bank[:, :].bitcast(F16).rearrange("p (j s f) -> p j s f", j=JC, s=2)

        s_gws, s_ow, s_bias, s_b2 = [sem(n) for n in ("s_gws", "s_ow", "s_bias", "s_b2")]
        s_gwp = [sem(f"s_gwp{k}") for k in range(2 * FT)]
        s_xt = [sem("s_xt0"), sem("s_xt1")]
        s_x = [sem(f"s_x{c}") for c in range(CH)]
        s_adj = [sem(f"s_adj{i}") for i in range(STG)]
        s_cast = sem("s_cast")
        s_const0, s_const = sem("s_const0"), sem("s_const")
        s_mx, s_mall = sem("s_mx"), sem("s_mall")
        s_sc = sem("s_sc")
        s_snh, s_snl = sem("s_snh"), sem("s_snl")
        s_vpart, s_vsum, s_vdeg = sem("s_vpart"), sem("s_vsum"), sem("s_vdeg")
        s_fold, s_fev = sem("s_fold"), sem("s_fev")
        s_wh, s_wl = sem("s_wh"), sem("s_wl")
        s_q0, s_q0h, s_q0l = sem("s_q0"), sem("s_q0h"), sem("s_q0l")
        s_p0, s_p0h, s_p0l = sem("s_p0"), sem("s_p0h"), sem("s_p0l")
        s_diag, s_dg, s_deg = sem("s_diag"), sem("s_dg"), sem("s_deg")
        s_pq, s_pqh, s_pql = sem("s_pq"), sem("s_pqh"), sem("s_pql")
        s_gate = sem("s_gate")
        s_c0, s_c1 = sem("s_c0"), sem("s_c1")
        s_pre = sem("s_pre")
        s_act = sem("s_act")
        s_rs, s_rsh, s_rsl = sem("s_rs"), sem("s_rsh"), sem("s_rsl")
        s_keep, s_zh, s_new = sem("s_keep"), sem("s_zh"), sem("s_new")
        s_sh, s_sl = sem("s_sh"), sem("s_sl")
        s_tr, s_nat = sem("s_tr"), sem("s_nat")
        s_cur = sem("s_cur")
        s_o1, s_hid, s_hh, s_hl = sem("s_o1"), sem("s_hid"), sem("s_hh"), sem("s_hl")
        s_o2, s_y, s_ln, s_norm = sem("s_o2"), sem("s_y"), sem("s_ln"), sem("s_norm")
        s_xr = [sem("s_xr0"), sem("s_xr1")]
        s_xb = sem("s_xb")
        s_out = [sem("s_out0"), sem("s_out1")]

        def cols(c):
            return slice(c * CW, (c + 1) * CW)

        def feat(f):
            return slice(f * P, (f + 1) * P)

        def head_rows(c, j):
            return bank[j][:, 0:D] if c == CH - 1 else bank[6 + j // 2][:, (j % 2) * D:(j % 2 + 1) * D]

        def p0_bank(c, f):
            return (2 * FT + 2 * c + f) % 8

        def store_rows(sp, c):
            for h in range(2):
                sp.wait_ge(s_norm, JC * c + 2 * h + 2)
                sp.dma_start(out.rearrange("(j p) f -> p j f", p=P)[:, c * JC + 2 * h:c * JC + 2 * h + 2, :],
                             y[:, c % 2, 2 * h:2 * h + 2, :]).then_inc(s_out[c % 2], 16)

        block = ctx.enter_context(nc.Block())

        @block.sync
        def _(sp):
            io_v = io_w.rearrange("(k p) m -> p k m", p=P)
            gw_v = gate_w.rearrange("(k p) m -> p k m", p=P)
            x_v = x.rearrange("(j p) f -> p j f", p=P)
            for d in range(2):
                for k in range(FT * d, FT * (d + 1)):
                    sp.dma_start(iow[:, k, :], io_v[:, k, :]).then_inc(s_gwp[k], 16)
                    sp.dma_start(gw[:, k, :], gw_v[:, k, :]).then_inc(s_gwp[k], 16)
            sp.dma_start(bias_sb[:, :], bias).then_inc(s_bias, 16)
            for c in range(CH):
                sp.dma_start(x_nat[:, c * JC:(c + 1) * JC, :], x_v[:, c * JC:(c + 1) * JC, :]) \
                    .then_inc(s_x[c], 16)

            def load_rows(k):
                src = adj if k < JT else adj_t
                if k >= STG:
                    sp.wait_ge(s_cast, k - STG + 1)
                sp.dma_start(stage[:, k % STG, :], src[(k % JT) * P:(k % JT + 1) * P, :]) \
                    .then_inc(s_adj[k % STG], 16)

            for k in range(2 * JT):
                load_rows(k)
                if k in (3, 5):
                    i = 2 * FT + (k - 3) // 2
                    sp.dma_start(gw[:, i, :], gw_v[:, i, :]).then_inc(s_gws, 16)
                if k == JT + 1:
                    sp.dma_start(ow, o_w.rearrange("(k p) m -> p k m", p=P)).then_inc(s_ow, 16)
                if k in (11, 15, 19, 23):
                    f, half = (k - 11) // 8, (k - 11) // 4 % 2
                    ns = slice(half * N // 2, (half + 1) * N // 2)
                    sp.dma_start(state_t[:, f, ns], x_t[f * P:(f + 1) * P, ns]).then_inc(s_xt[f], 16)

            sp.wait_ge(s_dg, 8)
            sp.dma_start(b2_all, o2_b.partition_broadcast(P)).then_inc(s_b2, 16)
            sp.wait_ge(s_gate, GT * CH)
            for c in range(CH):
                if c >= 2:
                    sp.wait_ge(s_out[c % 2], 32)
                sp.dma_start(y[:, c % 2, :, :], x_v[:, c * JC:(c + 1) * JC, :]).then_inc(s_xr[c % 2], 16)
                if c >= 1:
                    store_rows(sp, c - 1)
            store_rows(sp, CH - 1)
            sp.wait_ge(s_out[0], 16 * CH)
            sp.wait_ge(s_out[1], 16 * CH)

        @block.gpsimd
        def _(pool):
            nc.gpsimd.memset(ident[:, :], 0.0).then_inc(s_const0, 1)
            nc.gpsimd.memset(ones[:, :], 1.0).then_inc(s_const, 1)
            pool.wait_ge(s_const0, 1)
            nc.gpsimd.affine_select(out=ident[:, :], in_=ident[:, :], compare_op=ALU.not_equal, fill=1.0, base=0,
                                    pattern=[[-1, P]], channel_multiplier=1).then_inc(s_const, 1)
            pool.wait_ge(s_mx, 1)
            nc.gpsimd.partition_all_reduce(mall[:, 0:1], mx[:, 0:1], P, RMAX).then_inc(s_mall, 1)
            pool.wait_ge(s_mx, 2)
            nc.gpsimd.partition_all_reduce(mall[:, 1:3], mx[:, 1:3], P, RMAX).then_inc(s_mall, 1)
            pool.wait_ge(s_vpart, 4)
            nc.gpsimd.partition_all_reduce(v_sum[:, :, :], v_part[:, :, :], P, RADD).then_inc(s_vsum, 1)
            pool.wait_ge(s_mx, 3)
            nc.gpsimd.partition_all_reduce(mall[:, 3:5], mx[:, 3:5], P, RMAX).then_inc(s_mall, 1)
            pool.wait_ge(s_b2, 16)
            for c in range(CH):
                pool.wait_ge(s_xr[c % 2], 16 * (c // 2 + 1))
                for j in range(JC):
                    last = nc.gpsimd.tensor_tensor(y[:, c % 2, j, :], y[:, c % 2, j, :], b2_all, ALU.add)
                last.then_inc(s_xb, 1)

        @block.scalar
        def _(act):
            def fold_out(d):
                act.wait_ge(s_fold, d + 1)
                for k in range(FT):
                    nc.scalar.copy(fold[:, FT * d + k, 0:CW], bank[FT * d + k][:, :])
                    last = nc.scalar.copy(fold[:, FT * d + k, CW:GD], bank[4 + d][:, k * D:(k + 1) * D])
                last.then_inc(s_fev, 1)

            def cast_rows(k):
                act.wait_ge(s_adj[k % STG], 16 * (k // STG + 1))
                if k == JT + JT // 2:
                    act.wait_ge(s_vdeg, 1)
                dst = a8 if k < JT else at8
                nc.scalar.activation(dst[:, k % JT, :], stage[:, k % STG, :], ACT.Copy,
                                     accum_out=degc[:, k // JT, k % JT:k % JT + 1], saturate=False) \
                    .then_inc(s_cast, 1)

            fold_out(0)
            cast_rows(0)
            fold_out(1)
            for k in range(1, JT):
                cast_rows(k)
            act.wait_ge(s_wl, 2)
            cast_rows(JT)
            for c in range(CH):
                for f in range(FT):
                    act.wait_ge(s_q0, 2 * c + f + 1)
                    nc.scalar.activation(pq[:, c, FT + f, 0, :], bank[2 * c + f][:, :], ACT.Copy, scale=PSC) \
                        .then_inc(s_q0h, 1)
            for k in range(JT + 1, 2 * JT):
                cast_rows(k)
            for c in range(CH):
                for f in range(FT):
                    act.wait_ge(s_p0, 2 * c + f + 1)
                    nc.scalar.activation(pq[:, c, f, 0, :], bank[p0_bank(c, f)][:, :], ACT.Copy, scale=PSC) \
                        .then_inc(s_p0h, 1)

            def pq_hi(n, q):
                act.wait_ge(s_pq, 4 * (n - CH) + q + 1)
                nc.scalar.activation(pq[:, 0, q, 0, :], bank[q][:, :], ACT.Copy, scale=PSC).then_inc(s_pqh, 1)

            def nat_out(n, c, f, direct):
                dst = state_n if direct or c == CH - 1 else next_n
                act.wait_ge(s_tr, 2 * n + f + 1)
                nc.scalar.copy(dst[:, c * JC:(c + 1) * JC, :, feat(f)], tr16).then_inc(s_nat, 1)

            def gate_act(n, gi):
                dst = (r_buf, z_buf, h_buf)[gi // FT]
                act.wait_ge(s_pre, GT * n + gi + 1)
                nc.scalar.activation(dst[:, gi % FT, :], pre[:, gi % 3, :], ACT.Tanh if gi >= 2 * FT else ACT.Sigmoid,
                                     bias=bias_sb[:, 4 + gi:5 + gi], scale=UG).then_inc(s_act, 1)

            def gates(n, c, between=False):
                gate_act(n, 0)
                gate_act(n, 1)
                gate_act(n, 2)
                for f in range(FT):
                    gate_act(n, 3 + f)
                    if between:
                        nat_out(n - 1, c - 1, f, True)
                gate_act(n, 5)

            def head_act(c):
                for m in range(FT):
                    act.wait_ge(s_o1, FT * c + m + 1)
                    nc.scalar.activation(hid[:, m, :], bank[4 + m][:, :], ACT.Tanh,
                                         bias=bias_sb[:, 10 + m:11 + m], scale=UO1).then_inc(s_hid, 1)

            def step(t, last, first_direct):
                for c in range(CH):
                    n = CH * t + c
                    if c == 0:
                        nat_out(n - 1, CH - 1, 0, first_direct)
                        nat_out(n - 1, CH - 1, 1, first_direct)
                    pq_hi(n, 0)
                    if c > 0 and not last:
                        nat_out(n - 1, c - 1, 0, False)
                    if c > 0 and last:
                        head_act(c - 1)
                    pq_hi(n, 1)
                    if c > 0 and not last:
                        nat_out(n - 1, c - 1, 1, False)
                    pq_hi(n, 2)
                    pq_hi(n, 3)
                    gates(n, c)
                if last:
                    head_act(CH - 1)

            act.wait_ge(s_bias, 16)
            for c in range(CH):
                gates(c, c, between=c > 0)
            with act.Fori(1, STEPS - 1) as t:
                step(t, False, True)
            step(STEPS - 1, True, True)

        @block.vector
        def _(dve):
            chain = [0]

            def link(ins):
                chain[0] += 1
                ins.then_inc(s_sc, 1)
                dve.wait_ge(s_sc, chain[0])

            for c in range(CH):
                dve.wait_ge(s_x[c], 16)
                last = nc.vector.tensor_reduce(mx[:, 8 + c:9 + c], x_nat[:, c * JC:(c + 1) * JC, :],
                                               mybir.AxisListType.XY, ALU.max, apply_absolute_value=True)
            link(last)
            nc.vector.tensor_reduce(mx[:, 0:1], mx[:, 8:12], AX, ALU.max).then_inc(s_mx, 1)
            dve.wait_ge(s_mall, 1)
            link(nc.vector.tensor_scalar(T0, mall[:, 0:1], 1.0, None, ALU.max))
            link(nc.vector.tensor_scalar(PX.bitcast(U32), T0.bitcast(U32), EXP_BITS, None, ALU.bitwise_and))
            link(nc.vector.reciprocal(T1, PX))
            link(nc.vector.tensor_scalar(SIG, T1, TOP, None, ALU.mult))
            for c in range(CH):
                nc.vector.tensor_scalar(state_n[:, c * JC:(c + 1) * JC, 0, :], x_nat[:, c * JC:(c + 1) * JC, :], SIG,
                                        None, ALU.mult).then_inc(s_snh, 1)
                dve.wait_ge(s_snh, c + 1)
                for j in range(c * JC, (c + 1) * JC):
                    nc.vector.scalar_tensor_tensor(state_n[:, j, 1, :], x_nat[:, j, :], SIG, state_n[:, j, 0, :],
                                                   ALU.mult, ALU.subtract).then_inc(s_snl, 1)
            dve.wait_ge(s_bias, 16)
            for d in range(2):
                dve.wait_ge(s_gwp[FT * d], 32)
                nc.vector.tensor_scalar(v_part[:, d, :], gw[:, FT * d, :], bias_sb[:, FT * d:FT * d + 1], None,
                                        ALU.mult).then_inc(s_vpart, 1)
                dve.wait_ge(s_vpart, 2 * d + 1)
                dve.wait_ge(s_gwp[FT * d + 1], 32)
                nc.vector.scalar_tensor_tensor(v_part[:, d, :], gw[:, FT * d + 1, :],
                                               bias_sb[:, FT * d + 1:FT * d + 2], v_part[:, d, :],
                                               ALU.mult, ALU.add).then_inc(s_vpart, 1)
            dve.wait_ge(s_fev, 2)
            nc.vector.tensor_reduce(mx[:, 1:2], fold, mybir.AxisListType.XY, ALU.max, apply_absolute_value=True)
            dve.wait_ge(s_gws, 32)
            nc.vector.tensor_reduce(mx[:, 2:3], gw[:, 2 * FT:, :], mybir.AxisListType.XY, ALU.max,
                                    apply_absolute_value=True).then_inc(s_mx, 1)
            dve.wait_ge(s_mall, 2)
            link(nc.vector.tensor_scalar(T0, mall[:, 1:2], 1.0 / PSC, 1e-30, ALU.mult, ALU.max))
            link(nc.vector.tensor_tensor(T1, T0, mall[:, 2:3], ALU.max))
            link(nc.vector.tensor_scalar(PW.bitcast(U32), T1.bitcast(U32), EXP_BITS, None, ALU.bitwise_and))
            link(nc.vector.reciprocal(T0, PW))
            link(nc.vector.tensor_scalar(OMG, T0, TOP, None, ALU.mult))
            link(nc.vector.tensor_scalar(OMGP, T0, TOP / PSC, None, ALU.mult))
            link(nc.vector.tensor_scalar(UG, PW, PX, 1.0 / (TOP * TOP), ALU.mult, ALU.mult))

            def split_raw(done, dst, src, scale):
                nc.vector.tensor_scalar(dst[0], src, scale, None, ALU.mult).then_inc(s_wh, 1)
                dve.wait_ge(s_wh, done)
                nc.vector.scalar_tensor_tensor(dst[1], src, scale, dst[0], ALU.mult, ALU.subtract).then_inc(s_wl, 1)

            split_raw(1, [w16[:, 0:2 * FT, i, :] for i in range(2)], fold, OMGP)
            split_raw(2, [w16[:, 2 * FT:, i, :] for i in range(2)], gw[:, 2 * FT:, :], OMG)

            def lo_of_psum(c, q, src, done):
                return nc.vector.scalar_tensor_tensor(pq[:, c, q, 1, :], src[:, :], PSC, pq[:, c, q, 0, :],
                                                      ALU.mult, ALU.subtract).then_inc(done, 1)

            dve.wait_ge(s_const, 2)

            def make_diag(d):
                dve.wait_ge(s_cast, JT * (d + 1))
                for j in range(JT):
                    last = nc.vector.tensor_scalar(diag[:, d, j, :], ident[:, :], degc[:, d, j:j + 1], None, ALU.mult)
                last.then_inc(s_diag, 1)

            dve.wait_ge(s_vsum, 1)
            for d in range(2):
                for m in range(GT):
                    part = v_part[:, d, feat(m)]
                    last = nc.vector.scalar_tensor_tensor(part, v_sum[:, d, feat(m)], 1.0, ident[:, :],
                                                          ALU.mult, ALU.mult, accum_out=vdeg[:, d, m:m + 1])
            last.then_inc(s_vdeg, 1)
            dve.wait_ge(s_vdeg, 1)
            link(nc.vector.tensor_scalar(vdeg[:, :, :], vdeg[:, :, :], SIG, OMG, ALU.mult, ALU.mult))

            for c in range(CH):
                for f in range(FT):
                    dve.wait_ge(s_q0h, 2 * c + f + 1)
                    lo_of_psum(c, FT + f, bank[2 * c + f], s_q0l)
            make_diag(0)
            dve.wait_ge(s_ow, 16)
            nc.vector.tensor_reduce(mx[:, 3:4], ow[:, :, 0:D], mybir.AxisListType.XY, ALU.max,
                                    apply_absolute_value=True)
            nc.vector.tensor_reduce(mx[:, 4:5], ow[:, :, D:2 * D], mybir.AxisListType.XY, ALU.max,
                                    apply_absolute_value=True).then_inc(s_mx, 1)
            dve.wait_ge(s_mall, 3)
            for src, om, un in ((mall[:, 3:4], OM1, UO1), (mall[:, 4:5], OM2, UO2)):
                link(nc.vector.tensor_scalar(T0, src, 1e-30, None, ALU.max))
                link(nc.vector.tensor_scalar(un.bitcast(U32), T0.bitcast(U32), EXP_BITS, None, ALU.bitwise_and))
                link(nc.vector.reciprocal(T1, un))
                link(nc.vector.tensor_scalar(om, T1, TOP, None, ALU.mult))
            link(nc.vector.tensor_scalar(T0, UO1, PX, 1.0 / (TOP * TOP), ALU.mult, ALU.mult))
            link(nc.vector.tensor_copy(UO1, T0))
            link(nc.vector.tensor_scalar(T1, UO2, 1.0 / (TOP * TOP), None, ALU.mult))
            link(nc.vector.tensor_copy(UO2, T1))
            for i, om in enumerate((OM1, OM2)):
                ms = slice(i * D, (i + 1) * D)
                split_raw(3 + i, [o16[:, :, h, ms] for h in range(2)], ow[:, :, ms], om)
            for f in range(FT):
                dve.wait_ge(s_xt[f], 32)
                split_raw(5 + f, [split_t[:, h, f, :] for h in range(2)], state_t[:, f, :], SIG)
            make_diag(1)

            def p0_lo(c, f):
                dve.wait_ge(s_p0h, 2 * c + f + 1)
                lo_of_psum(c, f, bank[p0_bank(c, f)], s_p0l)

            def deg_out(d):
                for c in range(CH):
                    dve.wait_ge(s_dg, CH * d + c + 1)
                    nc.vector.tensor_copy(deg[:, d, cols(c)], bank[4 + c][:, :]).then_inc(s_deg, 1)

            for c in range(CH):
                p0_lo(c, 0)
                if c >= CH - 2:
                    deg_out(c - (CH - 2))
                p0_lo(c, 1)
            dve.wait_ge(s_deg, 2 * CH)

            def degree_part(n, c, gi):
                g = GT * n + gi
                slot = pre[:, gi % 3, :]
                if not (isinstance(n, int) and n == 0 and gi < 3):
                    dve.wait_ge(s_act, g - 2)
                nc.vector.tensor_scalar(slot, deg[:, 0, cols(c)], vdeg[:, 0, gi:gi + 1], None, ALU.mult) \
                    .then_inc(s_c0, 1)
                dve.wait_ge(s_c0, g + 1)
                nc.vector.scalar_tensor_tensor(slot, deg[:, 1, cols(c)], vdeg[:, 1, gi:gi + 1], slot,
                                               ALU.mult, ALU.add).then_inc(s_c1, 1)

            def gate_pre(n, gi):
                g = GT * n + gi
                slot = pre[:, gi % 3, :]
                dve.wait_ge(s_c1, g + 1)
                dve.wait_ge(s_gate, g + 1)
                nc.vector.tensor_tensor(slot, gate_bank[gi % 3][:, :], slot, ALU.add).then_inc(s_pre, 1)

            def split(dst, src, k, hi_done, lo_done, scale):
                nc.vector.tensor_scalar(dst[0], src, scale, None, ALU.mult).then_inc(hi_done, 1)
                dve.wait_ge(hi_done, k)
                nc.vector.scalar_tensor_tensor(dst[1], src, scale, dst[0], ALU.mult, ALU.subtract) \
                    .then_inc(lo_done, 1)

            def reset_part(n, c, f):
                k = FT * n + f + 1
                dve.wait_ge(s_act, GT * n + f + 1)
                nc.vector.tensor_tensor(r_buf[:, f, :], r_buf[:, f, :], state_t[:, f, cols(c)], ALU.mult) \
                    .then_inc(s_rs, 1)
                dve.wait_ge(s_rs, k)
                split([rs16[:, i, f, :] for i in range(2)], r_buf[:, f, :], k, s_rsh, s_rsl, SIG)

            def keep_part(n, c, f):
                dve.wait_ge(s_act, GT * n + 2 + f + 1)
                nc.vector.scalar_tensor_tensor(r_buf[:, f, :], z_buf[:, f, :], 1.0, state_t[:, f, cols(c)],
                                               ALU.subtract, ALU.mult).then_inc(s_keep, 1)

            def update(n, c, f):
                k = FT * n + f + 1
                dve.wait_ge(s_act, GT * n + 4 + f + 1)
                nc.vector.tensor_tensor(z_buf[:, f, :], z_buf[:, f, :], h_buf[:, f, :], ALU.mult).then_inc(s_zh, 1)
                dve.wait_ge(s_zh, k)
                dve.wait_ge(s_keep, k)
                nc.vector.tensor_tensor(state_t[:, f, cols(c)], z_buf[:, f, :], r_buf[:, f, :], ALU.subtract) \
                    .then_inc(s_new, 1)
                dve.wait_ge(s_new, k)
                split([split_t[:, i, f, cols(c)] for i in range(2)], state_t[:, f, cols(c)], k, s_sh, s_sl, SIG)

            def gates(n, c):
                for f in range(FT):
                    degree_part(n, c, f)
                for f in range(FT):
                    gate_pre(n, f)
                for f in range(FT):
                    reset_part(n, c, f)
                for f in range(FT):
                    degree_part(n, c, FT + f)
                    gate_pre(n, FT + f)
                for f in range(FT):
                    keep_part(n, c, f)
                for f in range(FT):
                    degree_part(n, c, 2 * FT + f)
                for f in range(FT):
                    gate_pre(n, 2 * FT + f)
                    update(n, c, f)

            def head_split(c):
                for m in range(FT):
                    dve.wait_ge(s_hid, FT * c + m + 1)
                    split([hid16[:, m, i, :] for i in range(2)], hid[:, m, :], FT * c + m + 1, s_hh, s_hl, TOP)

            ln_chain = [0]

            def ln_link(ins):
                ln_chain[0] += 1
                ins.then_inc(s_ln, 1)
                dve.wait_ge(s_ln, ln_chain[0])

            def statistics(c, j):
                dve.wait_ge(s_y, JC * c + j + 1)
                return nc.vector.bn_stats(ln_st[:, j, :], y[:, c % 2, j, :])

            def residual(c):
                dve.wait_ge(s_xb, c + 1)
                for j in range(JC):
                    if c == CH - 1 or j % 2 == 0:
                        dve.wait_ge(s_o2, 2 * c + 1 + (j if c == CH - 1 else j // 2))
                    rows = y[:, c % 2, j, :]
                    nc.vector.scalar_tensor_tensor(rows, head_rows(c, j), UO2, rows, ALU.mult, ALU.add) \
                        .then_inc(s_y, 1)
                    if j > 0:
                        statistics(c, j - 1)
                ln_link(statistics(c, JC - 1))

            def layer_norm(c):
                for j in range(JC):
                    last = nc.vector.bn_aggr(ln_mv[:, j, :], ln_st[:, j, :])
                ln_link(last)
                var, a, b, r = [ln_t[:, i, :] for i in range(4)]
                ln_link(nc.vector.tensor_scalar(var, ln_mv[:, :, 1], LN_EPS, None, ALU.add))
                ln_link(nc.vector.tensor_scalar(a.bitcast(U32), var.bitcast(U32), 1, None, ALU.logical_shift_right))
                ln_link(nc.vector.tensor_scalar(r.bitcast(I32), a.bitcast(I32), -1.0, float(0x5F3759DF),
                                                ALU.mult, ALU.add))
                for _ in range(NEWTON):
                    ln_link(nc.vector.tensor_tensor(a, r, r, ALU.mult))
                    ln_link(nc.vector.scalar_tensor_tensor(b, a, -0.5, var, ALU.mult, ALU.mult))
                    ln_link(nc.vector.scalar_tensor_tensor(r, b, 1.5, r, ALU.add, ALU.mult))
                for j in range(JC):
                    nc.vector.tensor_scalar(y[:, c % 2, j, :], y[:, c % 2, j, :], ln_mv[:, j, 0:1], ln_t[:, 3, j:j + 1],
                                            ALU.subtract, ALU.mult).then_inc(s_norm, 1)

            def pq_lo(n, q):
                dve.wait_ge(s_pqh, 4 * (n - CH) + q + 1)
                lo_of_psum(0, q, bank[q], s_pql)

            def step(t, last):
                for c in range(CH):
                    n = CH * t + c
                    pq_lo(n, 0)
                    if last and c > 0:
                        head_split(c - 1)
                    pq_lo(n, 1)
                    pq_lo(n, 2)
                    if last and c > 0:
                        residual(c - 1)
                        layer_norm(c - 1)
                    pq_lo(n, 3)
                    if c == CH - 1 and not last:
                        dve.wait_ge(s_nat, 2 * n)
                        nc.vector.tensor_copy(state_n[:, 0:JH, :, :], next_n).then_inc(s_cur, 1)
                    gates(n, c)
                if last:
                    head_split(CH - 1)
                    residual(CH - 1)
                    layer_norm(CH - 1)

            for c in range(CH):
                gates(c, c)
            with dve.Fori(1, STEPS - 1) as t:
                step(t, False)
            step(STEPS - 1, True)

        @block.tensor
        def _(pe):
            for d in range(2):
                wide = [(bank[FT * d + k][:, :], k, 0, CW) for k in range(FT)]
                narrow = [(bank[4 + d][:, k * D:(k + 1) * D], k, CW, GD) for k in range(FT)]
                order = [(p, ct) for ct in range(FT) for p in wide] + [(p, ct) for p in narrow for ct in range(FT)]
                for (dst, k, lo, hi), ct in order:
                    pe.wait_ge(s_gwp[FT * d + ct], 32)
                    last = nc.tensor.matmul(dst, iow[:, FT * d + ct, feat(k)], gw[:, FT * d + ct, lo:hi],
                                            start=ct == 0, stop=ct == FT - 1)
                last.then_inc(s_fold, 1)

            def adj_mm(dst, adj8, j, part, f, c):
                return nc.tensor.matmul(dst[:, :], state_n[:, j, part, feat(f)], adj8[:, j, cols(c)],
                                        start=j == 0 and part == 0, stop=j == JT - 1 and part == 1)

            pe.wait_ge(s_fev, 1)
            for j in range(JQ):
                pe.wait_ge(s_snl, j + 1)
                pe.wait_ge(s_cast, j + 1)
                for b in (0, 1, 4, 6, 7, 2, 3, 5):
                    if j == 0 and b == 2:
                        pe.wait_ge(s_fev, 2)
                    for part in range(2):
                        adj_mm(bank[b], a8, j, part, b % 2, b // 2)
            pe.wait_ge(s_snl, JT)
            pe.wait_ge(s_cast, JT)
            for c in range(CH):
                for f in range(FT):
                    for j in range(JQ, JT):
                        for part in range(2):
                            last = adj_mm(bank[2 * c + f], a8, j, part, f, c)
                    last.then_inc(s_q0, 1)
            for j in range(JQ):
                pe.wait_ge(s_cast, JT + j + 1)
                for c in (2, 3, 0, 1):
                    for f in range(FT):
                        if j == 0:
                            pe.wait_ge(s_q0h, p0_bank(c, f) + 1)
                            pe.wait_ge(s_q0l, p0_bank(c, f) + 1)
                        for part in range(2):
                            adj_mm(bank[p0_bank(c, f)], at8, j, part, f, c)
            pe.wait_ge(s_cast, 2 * JT)

            def spread_degrees(d):
                pe.wait_ge(s_diag, d + 1)
                for c in range(CH):
                    if d == 0:
                        pe.wait_ge(s_p0h, c + 1)
                        pe.wait_ge(s_p0l, c + 1)
                    else:
                        pe.wait_ge(s_deg, c + 1)
                    nc.tensor.matmul(bank[4 + c][:, :], ones[:, :], diag[:, d, c * JC:(c + 1) * JC, :],
                                     start=True, stop=True).then_inc(s_dg, 1)

            pe.wait_ge(s_const, 2)
            for c in range(CH):
                for f in range(FT):
                    for j in range(JQ, JT):
                        for part in range(2):
                            last = adj_mm(bank[p0_bank(c, f)], at8, j, part, f, c)
                    last.then_inc(s_p0, 1)
                    if c >= CH - 2 and f == 0:
                        spread_degrees(c - (CH - 2))

            def products(n, c, q, tiles):
                for j in tiles:
                    for part in range(2):
                        last = adj_mm(bank[q], (at8, a8)[q // FT], j, part, q % FT, c)
                if tiles[-1] == JT - 1:
                    last.then_inc(s_pq, 1)

            def gate_tile(n, c, gi, slot, ready):
                dst = gate_bank[gi % 3]
                adj_k = [0, 1, 2, 3]
                state_k = [4, 5]
                order = state_k + adj_k if gi < 2 * FT else adj_k + state_k
                for i, k in enumerate(order):
                    if k < 2 * FT and gi == 0:
                        ready(k)
                    if k >= 2 * FT and gi == 2 * FT:
                        pe.wait_ge(s_rsl, FT * n + k - 2 * FT + 1)
                    for wp, xp in PASSES:
                        if k < 2 * FT:
                            rhs = pq[:, slot, k, xp, :]
                        elif gi < 2 * FT:
                            rhs = split_t[:, xp, k - 2 * FT, cols(c)]
                        else:
                            rhs = rs16[:, xp, k - 2 * FT, :]
                        last = nc.tensor.matmul(dst[:, :], w16[:, k, wp, feat(gi)], rhs,
                                                start=i == 0 and (wp, xp) == PASSES[0],
                                                stop=i == KT - 1 and (wp, xp) == PASSES[-1])
                last.then_inc(s_gate, 1)

            def transposes(n, c, f):
                pe.wait_ge(s_sl, FT * n + f + 1)
                if isinstance(n, int) and n == 0 and f == 0:
                    pe.wait_ge(s_deg, 2 * CH)
                else:
                    pe.wait_ge(s_nat, 2 * n + f)
                for j in range(JC):
                    for part in range(2):
                        last = nc.tensor.transpose(tr16[:, j, part, :],
                                                   split_t[:, part, f, c * CW + j * P:c * CW + (j + 1) * P],
                                                   ident[:, :])
                last.then_inc(s_tr, 1)

            def head_hidden(c):
                n = CH * (STEPS - 1) + c
                for k in range(FT):
                    pe.wait_ge(s_sl, FT * n + k + 1)
                    for m in range(FT):
                        for wp, xp in PASSES:
                            last = nc.tensor.matmul(bank[4 + m][:, :], o16[:, k, wp, feat(m)],
                                                    split_t[:, xp, k, cols(c)],
                                                    start=k == 0 and (wp, xp) == PASSES[0],
                                                    stop=k == FT - 1 and (wp, xp) == PASSES[-1])
                        if k == FT - 1:
                            last.then_inc(s_o1, 1)

            def head_out(c):
                if 0 < c < CH - 1:
                    pe.wait_ge(s_y, JC * c)
                groups = [[(j, k)] for j in range(JC) for k in range(FT)] if c < CH - 1 else \
                    [[(j, k) for j in range(JC)] for k in range(FT)]
                for group in groups:
                    for j, k in group:
                        if j == 0:
                            pe.wait_ge(s_hl, FT * c + k + 1)
                        for wp, xp in PASSES:
                            last = nc.tensor.matmul(head_rows(c, j), hid16[:, k, xp, j * P:(j + 1) * P],
                                                    o16[:, k, wp, D:2 * D],
                                                    start=k == 0 and (wp, xp) == PASSES[0],
                                                    stop=k == FT - 1 and (wp, xp) == PASSES[-1])
                        if k == FT - 1 and (c == CH - 1 or j % 2):
                            last.then_inc(s_o2, 1)

            def gates(n, c, slot, ready, last_step=False, between=None):
                for gi in range(GT):
                    if isinstance(n, int) and n == 0 and gi < 3:
                        pe.wait_ge(s_deg, CH + gi + 1)
                    else:
                        pe.wait_ge(s_pre, GT * n + gi - 2)
                    if last_step and c > 0 and gi < 2:
                        pe.wait_ge(s_hid, FT * (c - 1) + gi + 1)
                    if last_step and c > 0 and gi == 2:
                        pe.wait_ge(s_y, JC * c - 2)
                    gate_tile(n, c, gi, slot, ready)
                    if between:
                        between(gi)

            def step(t, last):
                for c in range(CH):
                    n = CH * t + c
                    if c == 0:
                        pe.wait_ge(s_nat, 2 * n)
                        pe.nop(nofuse=True)
                    for q in range(2 * FT):
                        products(n, c, q, range(JH if c == 0 else 0, JT))
                        if c > 0 and not last and q < FT:
                            transposes(n - 1, c - 1, q)
                        if c > 0 and last and q == 0:
                            head_hidden(c - 1)
                        if c > 0 and last and q == 2:
                            head_out(c - 1)

                    def ready(k):
                        pe.wait_ge(s_pqh, 4 * (n - CH) + k + 1)
                        pe.wait_ge(s_pql, 4 * (n - CH) + k + 1)

                    gates(n, c, 0, ready, last_step=last)
                if not last:
                    pe.wait_ge(s_cur, t)
                    pe.nop(nofuse=True)
                    start_step(n)

            def start_step(n):
                for q in range(2 * FT):
                    products(n + 1, 0, q, range(0, JH))
                    if q in (1, 2):
                        transposes(n, CH - 1, q - 1)

            pe.wait_ge(s_wl, 6)
            for c in range(CH):
                def ready(k):
                    if k < FT:
                        pe.wait_ge(s_p0h, 2 * c + k + 1)
                        pe.wait_ge(s_p0l, 2 * c + k + 1)

                def between(gi):
                    if c > 0 and gi in (3, 4):
                        transposes(c - 1, c - 1, gi - 3)

                gates(c, c, c, ready, between=between)
            pe.wait_ge(s_nat, 2 * (CH - 1))
            start_step(CH - 1)
            with pe.Fori(1, STEPS - 1) as t:
                step(t, False)
            step(STEPS - 1, True)
            head_hidden(CH - 1)
            head_out(CH - 1)


def kernel(x, adj, L0_gnn_in_W, L0_gnn_in_b, L0_gnn_out_W, L0_gnn_out_b, L0_gnn_r_W, L0_gnn_r_b, L0_gnn_z_W,
           L0_gnn_z_b, L0_gnn_h_W, L0_gnn_h_b, L0_gnn_o1_W, L0_gnn_o1_b, L0_gnn_o2_W, L0_gnn_o2_b):
    import numpy as np
    import concourse.bacc as bacc
    from concourse.bass_utils import run_bass_kernel_spmd

    x, adj = np.asarray(x), np.asarray(adj)
    gates = [np.asarray(w) for w in (L0_gnn_r_W, L0_gnn_z_W, L0_gnn_h_W)]
    biases = (L0_gnn_in_b, L0_gnn_out_b, L0_gnn_r_b, L0_gnn_z_b, L0_gnn_h_b, L0_gnn_o1_b)
    arrays = {
        "x": x,
        "x_t": x.T,
        "adj": adj,
        "adj_t": adj.T,
        "io_w": np.concatenate([np.asarray(L0_gnn_in_W), np.asarray(L0_gnn_out_W)], axis=0),
        "gate_w": np.concatenate([w.T for w in gates], axis=1),
        "o_w": np.concatenate([np.asarray(L0_gnn_o1_W).T, np.asarray(L0_gnn_o2_W).T], axis=1),
        "bias": np.concatenate([np.asarray(b).reshape(FT, P).T for b in biases], axis=1),
        "o2_b": np.asarray(L0_gnn_o2_b),
    }
    arrays = {name: np.ascontiguousarray(a) for name, a in arrays.items()}
    nc = bacc.Bacc("TRN2", target_bir_lowering=False, num_devices=1)
    args = [nc.dram_tensor(f"in_{name}", a.shape, mybir.dt.from_np(a.dtype), kind="ExternalInput").ap()
            for name, a in arrays.items()]
    out = nc.dram_tensor("out", (N, D), F32, kind="ExternalOutput").ap()
    gnn_program(nc, *args, out)
    r = run_bass_kernel_spmd(nc, [{f"in_{name}": a for name, a in arrays.items()}], core_ids=[0])
    return r.results[0]["out"]
```
